# Optimizing a Trainium2 kernel written in Bass

```python
import numpy as np
import jax
import jax.numpy as jnp

def _softmax(x, axis=-1):
    return jax.nn.softmax(x, axis=axis)

def _gelu(x):
    return jax.nn.gelu(x, approximate=True)

def _silu(x):
    return jax.nn.silu(x)

def _sigmoid(x):
    return jax.nn.sigmoid(x)

def _layernorm(x, axis=-1, eps=1e-05):
    m = jnp.mean(x, axis=axis, keepdims=True)
    v = jnp.var(x, axis=axis, keepdims=True)
    return (x - m) / jnp.sqrt(v + eps)

def _scatter_add(tgt, idx, src, axis=0):
    return tgt.at[idx].add(src)

def _segment_sum(src, seg, n):
    return jax.ops.segment_sum(src, seg, n)
kernel_name = 'mk_rec_standalone_d1_rec_r8_53f3a9'

def setup_inputs(seed: int=0):
    np.random.seed(seed)
    _w = jnp.asarray

    def _rec_inputs():
        import jax
        import jax.numpy as jnp
        _rk = jax.random.key(seed)
        r_X_dense = -0.000171701 + 0.999137 * jax.random.normal(jax.random.fold_in(_rk, 1), (512, 13), jnp.float32)
        r_X_sparse = jnp.stack([jax.random.randint(jax.random.fold_in(jax.random.fold_in(_rk, 2), 0), (512,), 1, 1000, jnp.int32), jax.random.randint(jax.random.fold_in(jax.random.fold_in(_rk, 2), 1), (512,), 0, 7999, jnp.int32), jax.random.randint(jax.random.fold_in(jax.random.fold_in(_rk, 2), 2), (512,), 7, 7999, jnp.int32), jax.random.randint(jax.random.fold_in(jax.random.fold_in(_rk, 2), 3), (512,), 2, 7999, jnp.int32), jax.random.randint(jax.random.fold_in(jax.random.fold_in(_rk, 2), 4), (512,), 1, 1000, jnp.int32), jax.random.randint(jax.random.fold_in(jax.random.fold_in(_rk, 2), 5), (512,), 4, 1000, jnp.int32), jax.random.randint(jax.random.fold_in(jax.random.fold_in(_rk, 2), 6), (512,), 2, 7991, jnp.int32), jax.random.randint(jax.random.fold_in(jax.random.fold_in(_rk, 2), 7), (512,), 1, 7998, jnp.int32), jax.random.randint(jax.random.fold_in(jax.random.fold_in(_rk, 2), 8), (512,), 4, 7999, jnp.int32), jax.random.randint(jax.random.fold_in(jax.random.fold_in(_rk, 2), 9), (512,), 0, 1000, jnp.int32), jax.random.randint(jax.random.fold_in(jax.random.fold_in(_rk, 2), 10), (512,), 2, 999, jnp.int32), jax.random.randint(jax.random.fold_in(jax.random.fold_in(_rk, 2), 11), (512,), 0, 1000, jnp.int32), jax.random.randint(jax.random.fold_in(jax.random.fold_in(_rk, 2), 12), (512,), 1, 1000, jnp.int32), jax.random.randint(jax.random.fold_in(jax.random.fold_in(_rk, 2), 13), (512,), 0, 1000, jnp.int32), jax.random.randint(jax.random.fold_in(jax.random.fold_in(_rk, 2), 14), (512,), 1, 1000, jnp.int32), jax.random.randint(jax.random.fold_in(jax.random.fold_in(_rk, 2), 15), (512,), 1, 1000, jnp.int32), jax.random.randint(jax.random.fold_in(jax.random.fold_in(_rk, 2), 16), (512,), 1, 1000, jnp.int32), jax.random.randint(jax.random.fold_in(jax.random.fold_in(_rk, 2), 17), (512,), 9, 1000, jnp.int32), jax.random.randint(jax.random.fold_in(jax.random.fold_in(_rk, 2), 18), (512,), 2, 1000, jnp.int32), jax.random.randint(jax.random.fold_in(jax.random.fold_in(_rk, 2), 19), (512,), 4, 1000, jnp.int32), jax.random.randint(jax.random.fold_in(jax.random.fold_in(_rk, 2), 20), (512,), 0, 7999, jnp.int32), jax.random.randint(jax.random.fold_in(jax.random.fold_in(_rk, 2), 21), (512,), 6, 1000, jnp.int32), jax.random.randint(jax.random.fold_in(jax.random.fold_in(_rk, 2), 22), (512,), 0, 1000, jnp.int32), jax.random.randint(jax.random.fold_in(jax.random.fold_in(_rk, 2), 23), (512,), 2, 7997, jnp.int32), jax.random.randint(jax.random.fold_in(jax.random.fold_in(_rk, 2), 24), (512,), 3, 7999, jnp.int32), jax.random.randint(jax.random.fold_in(jax.random.fold_in(_rk, 2), 25), (512,), 0, 7997, jnp.int32)], axis=1)
        return (r_X_dense, r_X_sparse)
    r_X_dense, r_X_sparse = _rec_inputs()

    def _L0_rec_setup():
        import jax, jax.numpy as jnp
        import numpy as np
        F = 26
        V_FIELD = 1000
        V = F * V_FIELD
        D_EMB = 16
        DNN_IN = F * F * D_EMB
        H1, H2 = (256, 128)
        BS = 512
        NUM_DENSE = 13
        EPS = 1e-05

        def _bn(x, g, b):
            m = jnp.mean(x, axis=0)
            v = jnp.var(x, axis=0)
            return (x - m) * jax.lax.rsqrt(v + EPS) * g + b
        key = jax.random.key(seed)
        ks = jax.random.split(key, 16)

        def n(k, shape, s=0.05):
            return jax.random.normal(k, shape, dtype=jnp.float32) * s
        return {'X_sparse': jax.random.randint(ks[0], (BS, F), 0, V_FIELD, dtype=jnp.int32), 'X_dense': jax.random.normal(ks[1], (BS, NUM_DENSE), dtype=jnp.float32), 'fm1_emb': n(ks[2], (V, 1)), 'bias': jnp.zeros((1,), jnp.float32), 'fm1_dense_W': n(ks[3], (1, NUM_DENSE)), 'fm1_dense_b': jnp.zeros((1,), jnp.float32), 'emb_tables': n(ks[4], (F, V, D_EMB)), 'dense_W': n(ks[5], (DNN_IN, NUM_DENSE)), 'dense_b': jnp.zeros((DNN_IN,), jnp.float32), 'W1': n(ks[6], (H1, DNN_IN)), 'b1': jnp.zeros((H1,), jnp.float32), 'g1': jnp.ones((H1,), jnp.float32), 'beta1': jnp.zeros((H1,), jnp.float32), 'W2': n(ks[7], (H2, H1)), 'b2': jnp.zeros((H2,), jnp.float32), 'g2': jnp.ones((H2,), jnp.float32), 'beta2': jnp.zeros((H2,), jnp.float32), 'Wout': n(ks[8], (1, H2)), 'bout': jnp.zeros((1,), jnp.float32)}
    _L0_rec_all = _L0_rec_setup()
    _L0_rec_in = {k: v for k, v in _L0_rec_all.items() if k in ('fm1_emb', 'bias', 'fm1_dense_W', 'fm1_dense_b', 'emb_tables', 'dense_W', 'dense_b', 'W1', 'b1', 'g1', 'beta1', 'W2', 'b2', 'g2', 'beta2', 'Wout', 'bout')}
    del _L0_rec_all
    return {'r_X_dense': r_X_dense, 'r_X_sparse': r_X_sparse, 'L0_rec_fm1_emb': _L0_rec_in['fm1_emb'], 'L0_rec_bias': _L0_rec_in['bias'], 'L0_rec_fm1_dense_W': _L0_rec_in['fm1_dense_W'], 'L0_rec_fm1_dense_b': _L0_rec_in['fm1_dense_b'], 'L0_rec_emb_tables': _L0_rec_in['emb_tables'], 'L0_rec_dense_W': _L0_rec_in['dense_W'], 'L0_rec_dense_b': _L0_rec_in['dense_b'], 'L0_rec_W1': _L0_rec_in['W1'], 'L0_rec_b1': _L0_rec_in['b1'], 'L0_rec_g1': _L0_rec_in['g1'], 'L0_rec_beta1': _L0_rec_in['beta1'], 'L0_rec_W2': _L0_rec_in['W2'], 'L0_rec_b2': _L0_rec_in['b2'], 'L0_rec_g2': _L0_rec_in['g2'], 'L0_rec_beta2': _L0_rec_in['beta2'], 'L0_rec_Wout': _L0_rec_in['Wout'], 'L0_rec_bout': _L0_rec_in['bout']}

def reference(r_X_dense, r_X_sparse, L0_rec_fm1_emb, L0_rec_bias, L0_rec_fm1_dense_W, L0_rec_fm1_dense_b, L0_rec_emb_tables, L0_rec_dense_W, L0_rec_dense_b, L0_rec_W1, L0_rec_b1, L0_rec_g1, L0_rec_beta1, L0_rec_W2, L0_rec_b2, L0_rec_g2, L0_rec_beta2, L0_rec_Wout, L0_rec_bout):
    import jax
    import jax.numpy as jnp

    def _L0_rec_ref(X_sparse, X_dense, fm1_emb, bias, fm1_dense_W, fm1_dense_b, emb_tables, dense_W, dense_b, W1, b1, g1, beta1, W2, b2, g2, beta2, Wout, bout):
        import jax, jax.numpy as jnp
        import numpy as np
        F = 26
        V_FIELD = 1000
        V = F * V_FIELD
        D_EMB = 16
        DNN_IN = F * F * D_EMB
        H1, H2 = (256, 128)
        BS = 512
        NUM_DENSE = 13
        EPS = 1e-05

        def _bn(x, g, b):
            m = jnp.mean(x, axis=0)
            v = jnp.var(x, axis=0)
            return (x - m) * jax.lax.rsqrt(v + EPS) * g + b
        offsets = (jnp.arange(F, dtype=X_sparse.dtype) * V_FIELD)[None, :]
        X = X_sparse + offsets
        fm1 = jnp.sum(fm1_emb[X], axis=1) + bias
        fm1 = fm1 + X_dense @ fm1_dense_W.T + fm1_dense_b
        E = emb_tables[:, X, :]
        A = jnp.transpose(E, (1, 0, 2, 3))
        P = A * jnp.swapaxes(A, 1, 2)
        mask = jnp.triu(jnp.ones((F, F), jnp.float32), 1)
        fm2 = jnp.einsum('bijd,ij->b', P, mask)[:, None]
        dnn = A.reshape(A.shape[0], DNN_IN)
        dnn = dnn + jax.nn.relu(X_dense @ dense_W.T + dense_b)
        h = jax.nn.relu(_bn(dnn @ W1.T + b1, g1, beta1))
        h = jax.nn.relu(_bn(h @ W2.T + b2, g2, beta2))
        out = h @ Wout.T + bout
        return jax.nn.sigmoid(fm1 + fm2 + out)
    y = _L0_rec_ref(r_X_sparse, r_X_dense, L0_rec_fm1_emb, L0_rec_bias, L0_rec_fm1_dense_W, L0_rec_fm1_dense_b, L0_rec_emb_tables, L0_rec_dense_W, L0_rec_dense_b, L0_rec_W1, L0_rec_b1, L0_rec_g1, L0_rec_beta1, L0_rec_W2, L0_rec_b2, L0_rec_g2, L0_rec_beta2, L0_rec_Wout, L0_rec_bout)
    return y

_drawn_inputs = setup_inputs


def setup_inputs(seed=0):
    import zlib

    import numpy as np

    out = dict(_drawn_inputs(seed))
    spreads = {'L0_rec_dense_b': (0.0, 0.1),
     'L0_rec_b1': (0.0, 0.8),
     'L0_rec_g1': (1.0, 0.2),
     'L0_rec_beta1': (0.0, 0.599),
     'L0_rec_b2': (0.0, 0.8),
     'L0_rec_g2': (1.0, 0.568),
     'L0_rec_beta2': (0.0, 0.666)}
    factors = {}
    for name, (base, spread) in spreads.items():
        noise = np.random.default_rng([zlib.crc32(name.encode()), seed]).standard_normal(out[name].shape)
        drawn = base * np.exp(spread * noise) if base else spread * noise
        out[name] = jnp.asarray(drawn.astype(out[name].dtype))
    for name, factor in factors.items():
        out[name] = (out[name] * factor).astype(out[name].dtype)
    return out
```

```python
from contextlib import ExitStack

import concourse.bass as bass
from concourse import mybir

F32 = mybir.dt.float32
F32R = mybir.dt.float32r
I32 = mybir.dt.int32
ALU = mybir.AluOpType
ACT = mybir.ActivationFunctionType
AX_X = mybir.AxisListType.X

P = 128
F = 26
D = 16
V_FIELD = 1000
V = F * V_FIELD
FD = F * D
ROW = FD + 1
K = F * FD
H1, H2 = 256, 128
B = 512
BT = B // P
ND = 13
NA = ND + 1
NX = ND + 3
Q = 32
EPS = 1e-5

CHUNKS = -(-K // P)
PAIRS = -(-CHUNKS // 2)
UNITS = F * BT

STAGE = 5
DNN_RING = 4
T_RING = 4
R_RING = 2
HL_RING = 3
W_RING = 3
DW_RING = 2
LEAD = 8
M_LAG = 2

KEEP, kept_vectors = [], 0
for a, b in ((0, 7), (7, 13), (13, 19), (19, 25)):
    KEEP.append((a, b, F - 1 - a, kept_vectors))
    kept_vectors += (b - a) * (F - 1 - a)
PIECES = [(j, n) for j in range(1, F) for n, blk in enumerate(KEEP) if blk[0] < j]


def chunk_rows(c):
    return min(P, K - c * P)


def units_for_chunk(c):
    return BT * ((c * P + chunk_rows(c) - 1) // FD + 1)


def units_issued(c):
    return 0 if c < 0 else min(UNITS, c * UNITS * P // K + LEAD)


def last_chunk_of_field(j):
    return (FD * (j + 1) - 1) // P


def tri_copies(j):
    return 2 * min(j + 1, F - 1)


def build(nc, x_dense, x_sparse, table, dense_w, w1, w1_last, w2, b1, b2, bn1, bn2, fm_col, w_out,
          ident_in, out):
    ctx = ExitStack()
    with ctx:
        def sb(name, shape, dt=F32):
            return ctx.enter_context(nc.sbuf_tensor(name, shape, dt))

        def pb(name, shape):
            return ctx.enter_context(nc.psum_tensor(name, shape, F32))

        def sem(name):
            return ctx.enter_context(nc.semaphore(name))

        idx_in = sb("idx_in", [P, BT * F], I32)
        idx_off = sb("idx_off", [P, BT * F], I32)
        idx_sum = sb("idx_sum", [P, BT * F], I32)
        idx_wrap = sb("idx_wrap", [P, BT * F])
        idx_pos = sb("idx_pos", [P, BT * F])
        idx = sb("idx", [P, BT * F], I32)
        stage = sb("stage", [P, STAGE, BT, ROW])
        kept = sb("kept", [P, BT, kept_vectors * D])
        dnn = sb("dnn", [P, BT, DNN_RING * FD])
        fm2_parts = sb("fm2_parts", [P, BT, len(PIECES)])
        fm1_parts = sb("fm1_parts", [P, BT, F])
        dnn_hi = sb("dnn_hi", [P, HL_RING, B], F32R)
        dnn_lo = sb("dnn_lo", [P, HL_RING, B], F32R)
        w_raw = sb("w_raw", [P, W_RING, 2 * H1])
        w_hi = sb("w_hi", [P, W_RING, 2 * H1], F32R)
        w_lo = sb("w_lo", [P, W_RING, 2 * H1], F32R)
        dw_raw = sb("dw_raw", [P, DW_RING, FD])
        dw = sb("dw", [P, DW_RING, FD], F32R)
        x_raw = dnn[:, BT - 1, DNN_RING * FD - B:]
        x_split = sb("x_split", [P, B], F32R)
        x_rows = sb("x_rows", [NX, B])
        ident = sb("ident", [P, P])
        ones = sb("ones", [1, B])
        b1_row = sb("b1_row", [1, H1])
        b2_row = sb("b2_row", [1, H2])
        bn1_sb = sb("bn1_sb", [P, 2, 2])
        bn2_sb = sb("bn2_sb", [P, 2, 1])
        fm_sb = sb("fm_sb", [NX, 1])
        w2_sb = sb("w2_sb", [P, 2, H2])
        wo_sb = sb("wo_sb", [P, 1])
        h1 = dnn[:, 0:2, 0:B]
        h2 = dnn[:, 2:3, 0:B]
        stats = sb("stats", [P, 3, 6])
        mv = sb("mv", [P, 3, 2])
        ve = sb("ve", [P, 3])
        rec = sb("rec", [P, 3])
        root = sb("root", [P, 3])
        nwt = sb("nwt", [P, 4, 3])
        scale = sb("scale", [P, 3])
        shift = sb("shift", [P, 3])
        msc = sb("msc", [P, 3])
        fm1_sum = sb("fm1_sum", [P, BT])
        fm2_sum = sb("fm2_sum", [P, BT])
        fm_sum = sb("fm_sum", [P, BT])
        z = sb("z", [P, BT])
        warm = sb("warm", [P, 1])
        y = sb("y", [P, BT])

        acc = [pb(f"acc{h}", [P, B]) for h in range(2)]
        turned = [pb(f"turned{n}", [P, B]) for n in range(T_RING)]
        dense_ps = [pb(f"dense_ps{n}", [P, B]) for n in range(R_RING)]
        h2_ps = turned[0]
        z_ps = turned[1][:, 0:BT]

        s_idx_in = sem("s_idx_in")
        s_x_in = sem("s_x_in")
        s_small_in = sem("s_small_in")
        s_zeroed = sem("s_zeroed")
        s_consts = sem("s_consts")
        s_off = sem("s_off")
        s_idx_sum = sem("s_idx_sum")
        s_idx_step = sem("s_idx_step")
        s_idx = sem("s_idx")
        s_x_hi = sem("s_x_hi")
        s_x_lo = sem("s_x_lo")
        s_gathered = [sem(f"s_gathered{n}") for n in range(STAGE)]
        s_w_raw = [sem(f"s_w_raw{n}") for n in range(W_RING)]
        s_dw_raw = [sem(f"s_dw_raw{n}") for n in range(DW_RING)]
        s_w_hi = sem("s_w_hi")
        s_w_lo = sem("s_w_lo")
        s_dw_hi = sem("s_dw_hi")
        s_dw_lo = sem("s_dw_lo")
        s_dense = sem("s_dense")
        s_dnn = sem("s_dnn")
        s_fm2 = sem("s_fm2")
        s_tri = sem("s_tri")
        s_fm1 = sem("s_fm1")
        s_turned = sem("s_turned")
        s_hi = sem("s_hi")
        s_lo = sem("s_lo")
        s_mult = sem("s_mult")
        s_step = sem("s_step")
        s_var = sem("s_var")
        s_root = sem("s_root")
        s_affine = sem("s_affine")
        s_h = sem("s_h")
        s_h2_ps = sem("s_h2_ps")
        s_z_ps = sem("s_z_ps")
        s_z = sem("s_z")
        s_y = sem("s_y")
        s_out = sem("s_out")
        s_dstep = sem("s_dstep")

        SMALL_LOADS = 9
        W_LAST = (CHUNKS - 1) // 2

        block = ctx.enter_context(nc.Block())

        @block.sync
        def _(sp):
            sp.dma_start(idx_in[:], x_sparse).then_inc(s_idx_in, 16)

            def load_dense_w(j):
                slot = j % DW_RING
                if j >= DW_RING:
                    sp.wait_ge(s_dw_lo, j - DW_RING + 1)
                for q in range(4):
                    sp.dma_start(dw_raw[Q * q:Q * q + NA, slot, :],
                                 dense_w[:, j * FD:(j + 1) * FD]).then_inc(s_dw_raw[slot], 16)

            def load_w1(p):
                slot = p % W_RING
                if p >= W_RING:
                    sp.wait_ge(s_w_lo, p - W_RING + 1)
                if p == W_LAST:
                    sp.dma_start(w_raw[0:chunk_rows(CHUNKS - 1), slot, 0:H1],
                                 w1_last).then_inc(s_w_raw[slot], 16)
                else:
                    sp.dma_start(w_raw[:, slot, :], w1[:, 2 * p * H1:(2 * p + 2) * H1]
                                 ).then_inc(s_w_raw[slot], 16)

            sp.wait_ge(s_zeroed, 2)
            for q in range(4):
                sp.dma_start(x_raw[Q * q:Q * q + NA, :], x_dense[0:NA, :]).then_inc(s_x_in, 16)
            load_dense_w(0)
            sp.dma_start(ident[:], ident_in).then_inc(s_small_in, 16)
            sp.dma_start(b1_row[:], b1).then_inc(s_small_in, 16)
            load_w1(0)
            load_dense_w(1)
            load_w1(1)
            for t, src in ((x_rows, x_dense), (b2_row, b2), (bn1_sb, bn1), (bn2_sb, bn2),
                           (fm_sb, fm_col), (w2_sb, w2), (wo_sb, w_out)):
                sp.dma_start(t[:], src).then_inc(s_small_in, 16)
            j, p = 2, 2
            while j < F or p < PAIRS:
                if p < PAIRS and (j >= F or 2 * (p + 2) * P < (j - 1) * FD - P):
                    load_w1(p)
                    p += 1
                else:
                    load_dense_w(j)
                    j += 1
            sp.wait_ge(s_y, 1)
            sp.dma_start(out, y[:]).then_inc(s_out, 16)
            sp.wait_ge(s_out, 16)

        @block.gpsimd
        def _(pool):
            nc.gpsimd.iota(idx_off[:].rearrange("p (t f) -> p t f", f=F), pattern=[[0, BT], [V_FIELD, F]], base=0,
                           channel_multiplier=0).then_inc(s_off, 1)
            pool.wait_ge(s_off, 1)
            pool.wait_ge(s_idx_in, 16)
            nc.gpsimd.tensor_tensor(idx_sum[:], idx_in[:], idx_off[:], ALU.add).then_inc(s_idx_sum, 1)
            pool.wait_ge(s_idx, 1)

            def gather(j):
                slot = j % STAGE
                if j >= STAGE:
                    done = j - STAGE + 1
                    pool.wait_ge(s_dnn, BT * done)
                    if done > 1:
                        pool.wait_ge(s_fm2, BT * (done - 1))
                    pool.wait_ge(s_tri, tri_copies(done - 1))
                    pool.wait_ge(s_fm1, done)
                for t in range(BT):
                    col = t * F + j
                    nc.gpsimd.indirect_dma_start(
                        out=stage[:, slot, t, :], out_offset=None, in_=table,
                        in_offset=bass.IndirectOffsetOnAxis(ap=idx[:, col:col + 1], axis=0),
                    ).then_inc(s_gathered[slot], 16)

            def split_w1(p):
                slot = p % W_RING
                rows, cols = (chunk_rows(CHUNKS - 1), H1) if p == W_LAST else (P, 2 * H1)
                pool.wait_ge(s_w_hi, p + 1)
                nc.gpsimd.tensor_tensor(w_lo[0:rows, slot, 0:cols], w_raw[0:rows, slot, 0:cols],
                                        w_hi[0:rows, slot, 0:cols].bitcast(F32), ALU.subtract
                                        ).then_inc(s_w_lo, 1)

            p = 0
            for j in range(F):
                gather(j)
                while p < PAIRS and (p < min(W_RING, j + 1)
                                     or 2 * p * P < (j - STAGE + 1) * FD + 3 * P):
                    split_w1(p)
                    p += 1
            while p < PAIRS:
                split_w1(p)
                p += 1

        @block.scalar
        def _(act):
            act.wait_ge(s_x_in, 64)
            nc.scalar.copy(x_split[:], x_raw).then_inc(s_x_hi, 1)

            def dense_hi(j):
                slot = j % DW_RING
                act.wait_ge(s_dw_raw[slot], 64 * (j // DW_RING + 1))
                if j >= DW_RING:
                    act.wait_ge(s_dense, BT * (j - DW_RING + 1))
                nc.scalar.copy(dw[:, slot, :], dw_raw[:, slot, :]).then_inc(s_dw_hi, 1)

            def w1_hi(p):
                slot = p % W_RING
                rows, cols = (chunk_rows(CHUNKS - 1), H1) if p == W_LAST else (P, 2 * H1)
                act.wait_ge(s_w_raw[slot], 16 * (p // W_RING + 1))
                if p >= W_RING:
                    act.wait_ge(s_mult, 2 * (p - W_RING + 1))
                nc.scalar.copy(w_hi[0:rows, slot, 0:cols], w_raw[0:rows, slot, 0:cols]
                               ).then_inc(s_w_hi, 1)

            def keep(j):
                slot = j % STAGE
                act.wait_ge(s_gathered[slot], 64 * (j // STAGE + 1))
                nc.scalar.copy(fm1_parts[:, :, j], stage[:, slot, :, FD]).then_inc(s_fm1, 1)
                if j == F - 1:
                    return
                a, _, width, off = next(blk for blk in KEEP if blk[0] <= j < blk[1])
                at = (off + (j - a) * width + (j - a)) * D
                n = (F - 1 - j) * D
                for t in (0, 2):
                    nc.scalar.copy(kept[:, t:t + 2, at:at + n],
                                   stage[:, slot, t:t + 2, (j + 1) * D:FD]).then_inc(s_tri, 1)

            def hi(c):
                rows = chunk_rows(c)
                act.wait_ge(s_turned, c + 1)
                if c >= HL_RING:
                    act.wait_ge(s_mult, c - HL_RING + 1)
                nc.scalar.copy(dnn_hi[0:rows, c % HL_RING, :], turned[c % T_RING][0:rows, :]
                               ).then_inc(s_hi, 1)

            dense_hi(0)
            dense_hi(1)
            w1_hi(0)
            w1_hi(1)
            j, p, f = 2, 2, 0
            for c in range(CHUNKS):
                while f < F and BT * f + 2 <= units_issued(c):
                    keep(f)
                    f += 1
                while j < F and BT * (j - DW_RING + 1) <= units_issued(c):
                    dense_hi(j)
                    j += 1
                hi(c)
                if p < PAIRS and 2 * p <= c + 2:
                    w1_hi(p)
                    p += 1

            def normalise(n, src, dst):
                nc.scalar.activation(dst, src, ACT.Relu, bias=shift[:, n:n + 1],
                                     scale=scale[:, n:n + 1]).then_inc(s_h, 1)

            act.wait_ge(s_var, 1)
            nc.scalar.activation(root[:, 0:2], rec[:, 0:2], ACT.Sqrt).then_inc(s_root, 1)
            act.wait_ge(s_affine, 1)
            for h in range(2):
                normalise(h, acc[h][:], h1[:, h, :])
            act.wait_ge(s_var, 2)
            nc.scalar.activation(root[:, 2:3], rec[:, 2:3], ACT.Sqrt).then_inc(s_root, 1)
            nc.scalar.activation(warm[:], ident[:, 0:1], ACT.Sigmoid).then_inc(s_step, 1)
            act.wait_ge(s_affine, 2)
            normalise(2, h2_ps[:], h2[:, 0, :])
            act.wait_ge(s_z, 1)
            nc.scalar.activation(y[:], z[:], ACT.Sigmoid).then_inc(s_y, 1)

        @block.vector
        def _(dve):
            nc.vector.memset(x_raw, 0.0).then_inc(s_zeroed, 1)
            nc.vector.memset(dw_raw[:], 0.0).then_inc(s_zeroed, 1)
            nc.vector.memset(ones[:], 1.0).then_inc(s_consts, 1)
            dve.wait_ge(s_idx_sum, 1)
            nc.vector.tensor_scalar(idx_wrap[:], idx_sum[:], 0.0, float(V), ALU.is_lt, ALU.mult
                                    ).then_inc(s_idx_step, 1)
            dve.wait_ge(s_idx_step, 1)
            nc.vector.tensor_tensor(idx_pos[:], idx_sum[:], idx_wrap[:], ALU.add
                                    ).then_inc(s_idx_step, 1)
            dve.wait_ge(s_idx_step, 2)
            nc.vector.tensor_scalar(idx[:], idx_pos[:], 0.0, float(V - 1), ALU.max, ALU.min
                                    ).then_inc(s_idx, 1)
            dve.wait_ge(s_x_hi, 1)
            for q in (1, 3):
                rows = slice(Q * q, Q * (q + 1))
                nc.vector.tensor_tensor(x_split[rows, :], x_raw[rows, :],
                                        x_split[rows, :].bitcast(F32), ALU.subtract
                                        ).then_inc(s_x_lo, 1)

            def dense_lo(j):
                slot, rows = j % DW_RING, slice(2 * Q, 4 * Q)
                dve.wait_ge(s_dw_hi, j + 1)
                nc.vector.tensor_tensor(dw[rows, slot, :], dw_raw[rows, slot, :],
                                        dw[rows, slot, :].bitcast(F32), ALU.subtract
                                        ).then_inc(s_dw_lo, 1)

            def make_dnn(u):
                j, t = divmod(u, BT)
                slot = j % STAGE
                dve.wait_ge(s_dense, u + 1)
                if t == 0:
                    dve.wait_ge(s_gathered[slot], 64 * (j // STAGE + 1))
                    if j >= DNN_RING:
                        dve.wait_ge(s_turned, last_chunk_of_field(j - DNN_RING) + 1)
                at = (j % DNN_RING) * FD
                nc.vector.scalar_tensor_tensor(
                    out=dnn[:, t, at:at + FD], in0=dense_ps[u % R_RING][:, 0:FD], scalar=0.0,
                    in1=stage[:, slot, t, 0:FD], op0=ALU.max, op1=ALU.add).then_inc(s_dnn, 1)

            def pairwise(u):
                j, t = divmod(u, BT)
                if j == 0:
                    return
                if t == 0:
                    dve.wait_ge(s_tri, tri_copies(j - 1))
                for m, (jj, n) in enumerate(PIECES):
                    if jj != j:
                        continue
                    a, b, width, off = KEEP[n]
                    b = min(b, j)
                    blk = kept[:, t, off * D:(off + (KEEP[n][1] - a) * width) * D].rearrange(
                        "p (i w) -> p i w", w=width * D)
                    at = (j - 1 - a) * D
                    earlier = blk[:, 0:b - a, at:at + D]
                    last = nc.vector.tensor_tensor_reduce(
                        earlier,
                        stage[:, j % STAGE, t, a * D:b * D].rearrange("p (i d) -> p i d", d=D),
                        earlier, 1.0, 0.0, ALU.mult, ALU.add,
                        fm2_parts[:, t, m:m + 1])
                last.then_inc(s_fm2, 1)

            def lo(c):
                rows = chunk_rows(c)
                dve.wait_ge(s_hi, c + 1)
                nc.vector.tensor_tensor(dnn_lo[0:rows, c % HL_RING, :],
                                        turned[c % T_RING][0:rows, :],
                                        dnn_hi[0:rows, c % HL_RING, :].bitcast(F32),
                                        ALU.subtract).then_inc(s_lo, 1)

            dense_lo(0)
            dense_lo(1)
            for c in range(CHUNKS):
                for u in range(units_issued(c - 1), units_issued(c)):
                    j, t = divmod(u, BT)
                    if t == BT - 2 and DW_RING <= j + 1 < F:
                        dense_lo(j + 1)
                    make_dnn(u)
                    pairwise(u)
                if c >= 1:
                    lo(c - 1)
            lo(CHUNKS - 1)

            steps = [0]

            def step(instruction):
                steps[0] += 1
                instruction.then_inc(s_dstep, 1)
                dve.wait_ge(s_dstep, steps[0])

            dve.wait_ge(s_fm1, F)
            nc.vector.reduce_sum(fm1_sum[:], fm1_parts[:], AX_X).then_inc(s_dstep, 1)
            nc.vector.reduce_sum(fm2_sum[:], fm2_parts[:], AX_X).then_inc(s_dstep, 1)
            steps[0] = 2
            dve.wait_ge(s_dstep, 2)
            step(nc.vector.tensor_tensor(fm_sum[:], fm1_sum[:], fm2_sum[:], ALU.add))
            dve.wait_ge(s_small_in, 16 * SMALL_LOADS)

            def batch_norm(a, b, sources, params, which):
                cols = slice(a, b)
                for n, src in zip(range(a, b), sources):
                    step(nc.vector.bn_stats(stats[:, n, :], src))
                    step(nc.vector.bn_aggr(mv[:, n, :], stats[:, n, :]))
                step(nc.vector.tensor_scalar(ve[:, cols], mv[:, cols, 1], EPS, None, ALU.add))
                nc.vector.reciprocal(rec[:, cols], ve[:, cols]).then_inc(s_var, 1)
                dve.wait_ge(s_root, which)
                r, v = root[:, cols], ve[:, cols]
                step(nc.vector.tensor_tensor(nwt[:, 0, cols], r, r, ALU.mult))
                step(nc.vector.scalar_tensor_tensor(out=nwt[:, 1, cols], in0=nwt[:, 0, cols],
                                                    scalar=-0.5, in1=v, op0=ALU.mult,
                                                    op1=ALU.mult))
                step(nc.vector.scalar_tensor_tensor(out=nwt[:, 2, cols], in0=nwt[:, 1, cols],
                                                    scalar=1.5, in1=r, op0=ALU.add,
                                                    op1=ALU.mult))
                step(nc.vector.tensor_tensor(scale[:, cols], nwt[:, 2, cols], params[:, 0, :],
                                             ALU.mult))
                step(nc.vector.tensor_tensor(msc[:, cols], mv[:, cols, 0], scale[:, cols],
                                             ALU.mult))
                nc.vector.tensor_tensor(shift[:, cols], params[:, 1, :], msc[:, cols],
                                        ALU.subtract).then_inc(s_affine, 1)

            dve.wait_ge(s_mult, CHUNKS)
            batch_norm(0, 2, [acc[0][:], acc[1][:]], bn1_sb, 1)
            dve.wait_ge(s_h2_ps, 1)
            batch_norm(2, 3, [h2_ps[:]], bn2_sb, 2)
            dve.wait_ge(s_z_ps, 1)
            nc.vector.tensor_tensor(z[:], z_ps, fm_sum[:], ALU.add).then_inc(s_z, 1)


        @block.tensor
        def _(pe):
            def dense(u):
                j, t = divmod(u, BT)
                if t == 0:
                    pe.wait_ge(s_dw_lo, j + 1)
                if u >= R_RING:
                    pe.wait_ge(s_dnn, u - R_RING + 1)
                nc.tensor.matmul(dense_ps[u % R_RING][:, 0:FD], x_split[:, t * P:(t + 1) * P],
                                 dw[:, j % DW_RING, :], start=True, stop=True
                                 ).then_inc(s_dense, 1)

            def turn(c):
                rows = chunk_rows(c)
                at = c * P % (DNN_RING * FD)
                pe.wait_ge(s_dnn, units_for_chunk(c))
                if c >= T_RING:
                    pe.wait_ge(s_lo, c - T_RING + 1)
                for t in range(BT):
                    last = nc.tensor.transpose(turned[c % T_RING][0:rows, t * P:(t + 1) * P],
                                               dnn[:, t, at:at + rows], ident[:])
                last.then_inc(s_turned, 1)

            def multiply(c):
                rows = chunk_rows(c)
                slot, pair = c % HL_RING, (c // 2) % W_RING
                pe.wait_ge(s_lo, c + 1)
                pe.wait_ge(s_w_lo, c // 2 + 1)
                for w, x in ((w_hi, dnn_hi), (w_lo, dnn_hi), (w_hi, dnn_lo)):
                    for h in range(2):
                        at = (c % 2) * H1 + h * P
                        last = nc.tensor.matmul(acc[h][:], w[0:rows, pair, at:at + P],
                                                x[0:rows, slot, :], start=False,
                                                stop=(c == CHUNKS - 1 and x is dnn_lo))
                last.then_inc(s_mult, 1)

            pe.wait_ge(s_small_in, 16 * SMALL_LOADS)
            pe.wait_ge(s_consts, 1)
            for h in range(2):
                nc.tensor.matmul(acc[h][:], b1_row[:, h * P:(h + 1) * P], ones[:],
                                 start=True, stop=False)
            pe.wait_ge(s_x_lo, 2)
            for c in range(CHUNKS + M_LAG):
                if c < CHUNKS:
                    for u in range(units_issued(c - 1), units_issued(c)):
                        dense(u)
                    turn(c)
                if c >= M_LAG:
                    multiply(c - M_LAG)

            nc.tensor.matmul(h2_ps[:], b2_row[:], ones[:], start=True, stop=False)
            for h in range(2):
                pe.wait_ge(s_h, h + 1)
                last = nc.tensor.matmul(h2_ps[:], w2_sb[:, h, :], h1[:, h, :], start=False,
                                        stop=(h == 1))
            last.then_inc(s_h2_ps, 1)
            pe.wait_ge(s_h, 3)
            for t in range(BT):
                cols = slice(t * P, (t + 1) * P)
                nc.tensor.matmul(z_ps[:, t:t + 1], x_rows[:, cols], fm_sb[:], start=True, stop=False)
                last = nc.tensor.matmul(z_ps[:, t:t + 1], h2[:, 0, cols], wo_sb[:], start=False,
                                        stop=True)
            last.then_inc(s_z_ps, 1)


def kernel(r_X_dense, r_X_sparse, L0_rec_fm1_emb, L0_rec_bias, L0_rec_fm1_dense_W,
           L0_rec_fm1_dense_b, L0_rec_emb_tables, L0_rec_dense_W, L0_rec_dense_b, L0_rec_W1,
           L0_rec_b1, L0_rec_g1, L0_rec_beta1, L0_rec_W2, L0_rec_b2, L0_rec_g2, L0_rec_beta2,
           L0_rec_Wout, L0_rec_bout):
    import numpy as np
    import concourse.bacc as bacc
    from concourse.bass_utils import run_bass_kernel_spmd

    def a(x):
        return np.asarray(x)

    w1_k = a(L0_rec_W1).reshape(H1, F, F, D).transpose(2, 1, 3, 0).reshape(K, H1)
    dense_k = a(L0_rec_dense_W).reshape(F, F, D, ND).transpose(1, 0, 2, 3).reshape(K, ND)
    dense_b = a(L0_rec_dense_b).reshape(F, F, D).transpose(1, 0, 2).reshape(1, K)
    whole = K // P
    arrays = {
        "x_dense": np.concatenate([a(r_X_dense).T, np.ones((3, B), np.float32)]),
        "x_sparse": a(r_X_sparse).reshape(BT, P, F).transpose(1, 0, 2).reshape(P, BT * F),
        "table": np.concatenate([a(L0_rec_emb_tables).transpose(1, 0, 2).reshape(V, FD),
                                 a(L0_rec_fm1_emb)], axis=1),
        "dense_w": np.concatenate([dense_k.T, dense_b]),
        "w1": w1_k[:whole * P].reshape(whole, P, H1).transpose(1, 0, 2).reshape(P, whole * H1),
        "w1_last": w1_k[whole * P:],
        "w2": a(L0_rec_W2).T.reshape(2, P, H2).transpose(1, 0, 2),
        "b1": a(L0_rec_b1).reshape(1, H1),
        "b2": a(L0_rec_b2).reshape(1, H2),
        "bn1": np.stack([a(L0_rec_g1).reshape(2, P).T, a(L0_rec_beta1).reshape(2, P).T], axis=1),
        "bn2": np.stack([a(L0_rec_g2), a(L0_rec_beta2)], axis=1).reshape(P, 2, 1),
        "fm_col": np.concatenate([a(L0_rec_fm1_dense_W).reshape(ND), a(L0_rec_fm1_dense_b),
                                  a(L0_rec_bias), a(L0_rec_bout)]).reshape(NX, 1),
        "w_out": a(L0_rec_Wout).reshape(H2, 1),
        "ident_in": np.eye(P, dtype=np.float32),
    }
    arrays = {n: np.ascontiguousarray(x) for n, x in arrays.items()}
    nc = bacc.Bacc("TRN2", target_bir_lowering=False, num_devices=1)
    args = {n: nc.dram_tensor(f"in_{n}", x.shape, mybir.dt.from_np(x.dtype), kind="ExternalInput").ap()
            for n, x in arrays.items()}
    result = nc.dram_tensor("out_y", (P, BT), F32, kind="ExternalOutput").ap()
    build(nc, **args, out=result)
    r = run_bass_kernel_spmd(nc, [{f"in_{n}": x for n, x in arrays.items()}], core_ids=[0])
    return np.asarray(r.results[0]["out_y"]).T.reshape(B, 1)
```

```python
from contextlib import ExitStack

import concourse.bass as bass
from concourse import mybir

F32 = mybir.dt.float32
F32R = mybir.dt.float32r
I32 = mybir.dt.int32
ALU = mybir.AluOpType
ACT = mybir.ActivationFunctionType
AX_X = mybir.AxisListType.X

P = 128
F = 26
D = 16
V_FIELD = 1000
V = F * V_FIELD
FD = F * D
ROW = FD + 1
K = F * FD
H1, H2 = 256, 128
B = 512
BT = B // P
ND = 13
NA = ND + 1
NX = ND + 3
Q = 32
EPS = 1e-5

CHUNKS = -(-K // P)
PAIRS = -(-CHUNKS // 2)
UNITS = F * BT

STAGE = 5
DNN_RING = 4
T_RING = 4
R_RING = 2
HL_RING = 3
W_RING = 3
DW_RING = 2
LEAD = 8
M_LAG = 2

KEEP, kept_vectors = [], 0
for a, b in ((0, 7), (7, 13), (13, 19), (19, 25)):
    KEEP.append((a, b, F - 1 - a, kept_vectors))
    kept_vectors += (b - a) * (F - 1 - a)
PIECES = [(j, n) for j in range(1, F) for n, blk in enumerate(KEEP) if blk[0] < j]


def chunk_rows(c):
    return min(P, K - c * P)


def units_for_chunk(c):
    return BT * ((c * P + chunk_rows(c) - 1) // FD + 1)


def units_issued(c):
    return 0 if c < 0 else min(UNITS, c * UNITS * P // K + LEAD, BT + 2 * c)


def last_chunk_of_field(j):
    return (FD * (j + 1) - 1) // P


def tri_copies(j):
    return 2 * min(j + 1, F - 1)


def build(nc, x_dense, x_sparse, table, dense_w, w1, w1_last, w2, b1, b2, bn1, bn2, fm_col, w_out,
          ident_in, out):
    ctx = ExitStack()
    with ctx:
        def sb(name, shape, dt=F32):
            return ctx.enter_context(nc.sbuf_tensor(name, shape, dt))

        def pb(name, shape):
            return ctx.enter_context(nc.psum_tensor(name, shape, F32))

        def sem(name):
            return ctx.enter_context(nc.semaphore(name))

        idx_in = sb("idx_in", [P, BT * F], I32)
        idx_off = sb("idx_off", [P, BT * F], I32)
        idx_sum = sb("idx_sum", [P, BT * F], I32)
        idx_wrap = sb("idx_wrap", [P, BT * F])
        idx_pos = sb("idx_pos", [P, BT * F])
        idx = sb("idx", [P, BT * F], I32)
        stage = sb("stage", [P, STAGE, BT, ROW])
        kept = sb("kept", [P, BT, kept_vectors * D])
        dnn = sb("dnn", [P, BT, DNN_RING * FD])
        fm2_parts = sb("fm2_parts", [P, BT, len(PIECES)])
        fm1_parts = sb("fm1_parts", [P, BT, F])
        dnn_hi = sb("dnn_hi", [P, HL_RING, B], F32R)
        dnn_lo = sb("dnn_lo", [P, HL_RING, B], F32R)
        w_raw = sb("w_raw", [P, W_RING, 2 * H1])
        w_hi = sb("w_hi", [P, W_RING, 2 * H1], F32R)
        w_lo = sb("w_lo", [P, W_RING, 2 * H1], F32R)
        dw_raw = sb("dw_raw", [P, DW_RING, FD])
        dw = sb("dw", [P, DW_RING, FD], F32R)
        x_raw = dnn[:, BT - 1, DNN_RING * FD - B:]
        x_split = sb("x_split", [P, B], F32R)
        x_rows = sb("x_rows", [NX, B])
        ident = sb("ident", [P, P])
        ones = sb("ones", [1, B])
        b1_row = sb("b1_row", [1, H1])
        b2_row = sb("b2_row", [1, H2])
        bn1_sb = sb("bn1_sb", [P, 2, 2])
        bn2_sb = sb("bn2_sb", [P, 2, 1])
        fm_sb = sb("fm_sb", [NX, 1])
        w2_sb = sb("w2_sb", [P, 2, H2])
        wo_sb = sb("wo_sb", [P, 1])
        h1 = dnn[:, 0:2, 0:B]
        h2 = dnn[:, 2:3, 0:B]
        stats = sb("stats", [P, 3, 6])
        mv = sb("mv", [P, 3, 2])
        ve = sb("ve", [P, 3])
        rec = sb("rec", [P, 3])
        root = sb("root", [P, 3])
        nwt = sb("nwt", [P, 3, 3])
        scale = sb("scale", [P, 3])
        shift = sb("shift", [P, 3])
        fm1_sum = sb("fm1_sum", [P, BT])
        fm2_sum = sb("fm2_sum", [P, BT])
        fm_sum = sb("fm_sum", [P, BT])
        fm_all = sb("fm_all", [P, BT])
        eps = sb("eps", [P, 1])
        z = sb("z", [P, BT])
        warm = sb("warm", [P, 2])
        y = sb("y", [P, BT])

        acc = [pb(f"acc{h}", [P, B]) for h in range(2)]
        turned = [pb(f"turned{n}", [P, B]) for n in range(T_RING)]
        dense_ps = [pb(f"dense_ps{n}", [P, B]) for n in range(R_RING)]
        h2_ps = turned[CHUNKS % T_RING]
        z_ps = dense_ps[0][:, 0:BT]
        first_ps = dense_ps[1][:, 0:BT]

        s_idx_in = sem("s_idx_in")
        s_x_in = sem("s_x_in")
        s_b1_in = sem("s_b1_in")
        s_ident_in = sem("s_ident_in")
        s_small_in = sem("s_small_in")
        s_zeroed = sem("s_zeroed")
        s_consts = sem("s_consts")
        s_off = sem("s_off")
        s_idx_sum = sem("s_idx_sum")
        s_idx_step = sem("s_idx_step")
        s_idx = sem("s_idx")
        s_x_hi = sem("s_x_hi")
        s_x_lo = sem("s_x_lo")
        s_gathered = [[sem(f"s_gathered{n}_{t}") for t in range(BT)] for n in range(STAGE)]
        s_w_raw = [sem(f"s_w_raw{n}") for n in range(W_RING)]
        s_dw_raw = [sem(f"s_dw_raw{n}") for n in range(DW_RING)]
        s_w_hi = sem("s_w_hi")
        s_w_lo = sem("s_w_lo")
        s_dw_hi = sem("s_dw_hi")
        s_dw_lo = sem("s_dw_lo")
        s_dense = sem("s_dense")
        s_dnn = sem("s_dnn")
        s_fm2 = sem("s_fm2")
        s_tri = sem("s_tri")
        s_fm1 = sem("s_fm1")
        s_turned = sem("s_turned")
        s_hi = sem("s_hi")
        s_lo = sem("s_lo")
        s_mult = sem("s_mult")
        s_warm = sem("s_warm")
        s_acc = sem("s_acc")
        s_first_ps = sem("s_first_ps")
        s_var = sem("s_var")
        s_root = sem("s_root")
        s_affine = sem("s_affine")
        s_h = sem("s_h")
        s_h2_ps = sem("s_h2_ps")
        s_z_ps = sem("s_z_ps")
        s_z = sem("s_z")
        s_y = sem("s_y")
        s_out = sem("s_out")
        s_dstep = sem("s_dstep")

        SMALL_LOADS = 7
        W_LAST = (CHUNKS - 1) // 2

        block = ctx.enter_context(nc.Block())

        @block.sync
        def _(sp):
            sp.dma_start(idx_in[:], x_sparse).then_inc(s_idx_in, 16)

            def load_dense_w(j):
                slot = j % DW_RING
                if j >= DW_RING:
                    sp.wait_ge(s_dw_lo, j - DW_RING + 1)
                for q in range(4):
                    sp.dma_start(dw_raw[Q * q:Q * q + NA, slot, :],
                                 dense_w[:, j * FD:(j + 1) * FD]).then_inc(s_dw_raw[slot], 16)

            def load_w1(p):
                slot = p % W_RING
                if p >= W_RING:
                    sp.wait_ge(s_w_lo, p - W_RING + 1)
                if p == W_LAST:
                    sp.dma_start(w_raw[0:chunk_rows(CHUNKS - 1), slot, 0:H1],
                                 w1_last).then_inc(s_w_raw[slot], 16)
                else:
                    sp.dma_start(w_raw[:, slot, :], w1[:, 2 * p * H1:(2 * p + 2) * H1]
                                 ).then_inc(s_w_raw[slot], 16)

            sp.wait_ge(s_zeroed, 1)
            for q in range(4):
                sp.dma_start(x_raw[Q * q:Q * q + NA, :], x_dense[0:NA, :]).then_inc(s_x_in, 16)
            sp.wait_ge(s_zeroed, 2)
            load_dense_w(0)
            sp.dma_start(b1_row[:], b1).then_inc(s_b1_in, 16)
            load_w1(0)
            sp.dma_start(ident[:], ident_in).then_inc(s_ident_in, 16)
            sp.wait_ge(s_zeroed, 3)
            load_dense_w(1)
            load_w1(1)
            load_w1(2)
            for t, src in ((x_rows, x_dense), (b2_row, b2), (bn1_sb, bn1), (bn2_sb, bn2),
                           (fm_sb, fm_col), (w2_sb, w2), (wo_sb, w_out)):
                sp.dma_start(t[:], src).then_inc(s_small_in, 16)
            j, p = 2, 3
            while j < F or p < PAIRS:
                if p < PAIRS and (j >= F or 2 * (p + 2) * P < (j - 1) * FD - P):
                    load_w1(p)
                    p += 1
                else:
                    load_dense_w(j)
                    j += 1
            sp.wait_ge(s_y, 1)
            sp.dma_start(out, y[:]).then_inc(s_out, 16)
            sp.wait_ge(s_out, 16)

        @block.gpsimd
        def _(pool):
            nc.gpsimd.iota(idx_off[:].rearrange("p (t f) -> p t f", f=F), pattern=[[0, BT], [V_FIELD, F]], base=0,
                           channel_multiplier=0).then_inc(s_off, 1)
            pool.wait_ge(s_off, 1)
            pool.wait_ge(s_idx_in, 16)
            nc.gpsimd.tensor_tensor(idx_sum[:], idx_in[:], idx_off[:], ALU.add).then_inc(s_idx_sum, 1)
            pool.wait_ge(s_idx, 1)

            def gather(j):
                slot = j % STAGE
                if j >= STAGE:
                    done = j - STAGE + 1
                    pool.wait_ge(s_dnn, BT * done)
                    if done > 1:
                        pool.wait_ge(s_fm2, BT * (done - 1))
                    pool.wait_ge(s_tri, tri_copies(done - 1))
                    pool.wait_ge(s_fm1, done)
                for t in range(BT):
                    col = t * F + j
                    nc.gpsimd.indirect_dma_start(
                        out=stage[:, slot, t, :], out_offset=None, in_=table,
                        in_offset=bass.IndirectOffsetOnAxis(ap=idx[:, col:col + 1], axis=0),
                    ).then_inc(s_gathered[slot][t], 16)

            def split_w1(p):
                slot = p % W_RING
                rows, cols = (chunk_rows(CHUNKS - 1), H1) if p == W_LAST else (P, 2 * H1)
                pool.wait_ge(s_w_hi, p + 1)
                nc.gpsimd.tensor_tensor(w_lo[0:rows, slot, 0:cols], w_raw[0:rows, slot, 0:cols],
                                        w_hi[0:rows, slot, 0:cols].bitcast(F32), ALU.subtract
                                        ).then_inc(s_w_lo, 1)

            p = 0
            for j in range(F):
                gather(j)
                while p < PAIRS and (p < min(W_RING, j)
                                     or 2 * p * P < (j - STAGE + 1) * FD + 3 * P):
                    split_w1(p)
                    p += 1
            while p < PAIRS:
                split_w1(p)
                p += 1

        @block.scalar
        def _(act):
            act.wait_ge(s_x_in, 64)
            nc.scalar.copy(x_split[:], x_raw).then_inc(s_x_hi, 1)

            def dense_hi(j):
                slot = j % DW_RING
                act.wait_ge(s_dw_raw[slot], 64 * (j // DW_RING + 1))
                if j >= DW_RING:
                    act.wait_ge(s_dense, BT * (j - DW_RING + 1))
                nc.scalar.copy(dw[:, slot, :], dw_raw[:, slot, :]).then_inc(s_dw_hi, 1)

            def w1_hi(p):
                slot = p % W_RING
                rows, cols = (chunk_rows(CHUNKS - 1), H1) if p == W_LAST else (P, 2 * H1)
                act.wait_ge(s_w_raw[slot], 16 * (p // W_RING + 1))
                if p >= W_RING:
                    act.wait_ge(s_mult, 2 * (p - W_RING + 1))
                nc.scalar.copy(w_hi[0:rows, slot, 0:cols], w_raw[0:rows, slot, 0:cols]
                               ).then_inc(s_w_hi, 1)

            def keep(j):
                slot = j % STAGE
                for t in range(BT):
                    act.wait_ge(s_gathered[slot][t], 16 * (j // STAGE + 1))
                nc.scalar.copy(fm1_parts[:, :, j], stage[:, slot, :, FD]).then_inc(s_fm1, 1)
                if j == F - 1:
                    return
                a, _, width, off = next(blk for blk in KEEP if blk[0] <= j < blk[1])
                at = (off + (j - a) * width + (j - a)) * D
                n = (F - 1 - j) * D
                for t in (0, 2):
                    nc.scalar.copy(kept[:, t:t + 2, at:at + n],
                                   stage[:, slot, t:t + 2, (j + 1) * D:FD]).then_inc(s_tri, 1)

            def hi(c):
                rows = chunk_rows(c)
                act.wait_ge(s_turned, c + 1)
                if c >= HL_RING:
                    act.wait_ge(s_mult, c - HL_RING + 1)
                nc.scalar.copy(dnn_hi[0:rows, c % HL_RING, :], turned[c % T_RING][0:rows, :]
                               ).then_inc(s_hi, 1)

            dense_hi(0)
            dense_hi(1)
            w1_hi(0)
            w1_hi(1)
            j, p, f = 2, 2, 0
            for c in range(CHUNKS):
                while f < F and BT * f + 2 <= units_issued(c):
                    keep(f)
                    f += 1
                while j < F and BT * (j - DW_RING + 1) <= units_issued(c):
                    dense_hi(j)
                    j += 1
                hi(c)
                if p < PAIRS and 2 * p <= c + 2:
                    w1_hi(p)
                    p += 1

            def normalise(n, src, dst):
                nc.scalar.activation(dst, src, ACT.Relu, bias=shift[:, n:n + 1],
                                     scale=scale[:, n:n + 1]).then_inc(s_h, 1)

            act.wait_ge(s_consts, 2)
            nc.scalar.activation(warm[:, 0:1], eps[:], ACT.Sqrt).then_inc(s_warm, 1)
            for h in range(2):
                act.wait_ge(s_var, h + 1)
                nc.scalar.activation(root[:, h:h + 1], mv[:, h, 1:2], ACT.Sqrt, bias=eps[:]
                                     ).then_inc(s_root, 1)
            for h in range(2):
                act.wait_ge(s_affine, h + 1)
                normalise(h, acc[h][:], h1[:, h, :])
            act.wait_ge(s_var, 3)
            nc.scalar.activation(root[:, 2:3], mv[:, 2, 1:2], ACT.Sqrt, bias=eps[:]
                                 ).then_inc(s_root, 1)
            nc.scalar.activation(warm[:, 1:2], eps[:], ACT.Sigmoid).then_inc(s_warm, 1)
            act.wait_ge(s_affine, 3)
            normalise(2, h2_ps[:], h2[:, 0, :])
            act.wait_ge(s_z, 1)
            nc.scalar.activation(y[:], z[:], ACT.Sigmoid).then_inc(s_y, 1)

        @block.vector
        def _(dve):
            nc.vector.memset(x_raw, 0.0).then_inc(s_zeroed, 1)
            for n in range(DW_RING):
                nc.vector.memset(dw_raw[:, n, :], 0.0).then_inc(s_zeroed, 1)
            dve.wait_ge(s_idx_sum, 1)
            nc.vector.tensor_scalar(idx_wrap[:], idx_sum[:], 0.0, float(V), ALU.is_lt, ALU.mult
                                    ).then_inc(s_idx_step, 1)
            dve.wait_ge(s_idx_step, 1)
            nc.vector.tensor_tensor(idx_pos[:], idx_sum[:], idx_wrap[:], ALU.add
                                    ).then_inc(s_idx_step, 1)
            dve.wait_ge(s_idx_step, 2)
            nc.vector.tensor_scalar(idx[:], idx_pos[:], 0.0, float(V - 1), ALU.max, ALU.min
                                    ).then_inc(s_idx, 1)
            nc.vector.memset(ones[:], 1.0).then_inc(s_consts, 1)
            nc.vector.memset(eps[:], EPS).then_inc(s_consts, 1)
            dve.wait_ge(s_x_hi, 1)
            for q in (1, 3):
                rows = slice(Q * q, Q * (q + 1))
                nc.vector.tensor_tensor(x_split[rows, :], x_raw[rows, :],
                                        x_split[rows, :].bitcast(F32), ALU.subtract
                                        ).then_inc(s_x_lo, 1)

            def dense_lo(j):
                slot, rows = j % DW_RING, slice(2 * Q, 4 * Q)
                dve.wait_ge(s_dw_hi, j + 1)
                nc.vector.tensor_tensor(dw[rows, slot, :], dw_raw[rows, slot, :],
                                        dw[rows, slot, :].bitcast(F32), ALU.subtract
                                        ).then_inc(s_dw_lo, 1)

            def make_dnn(u):
                j, t = divmod(u, BT)
                slot = j % STAGE
                dve.wait_ge(s_dense, u + 1)
                dve.wait_ge(s_gathered[slot][t], 16 * (j // STAGE + 1))
                if t == 0 and j >= DNN_RING:
                    dve.wait_ge(s_turned, last_chunk_of_field(j - DNN_RING) + 1)
                at = (j % DNN_RING) * FD
                nc.vector.scalar_tensor_tensor(
                    out=dnn[:, t, at:at + FD], in0=dense_ps[u % R_RING][:, 0:FD], scalar=0.0,
                    in1=stage[:, slot, t, 0:FD], op0=ALU.max, op1=ALU.add).then_inc(s_dnn, 1)

            def pairwise(u):
                j, t = divmod(u, BT)
                if j == 0:
                    return
                if t == 0:
                    dve.wait_ge(s_tri, tri_copies(j - 1))
                for m, (jj, n) in enumerate(PIECES):
                    if jj != j:
                        continue
                    a, b, width, off = KEEP[n]
                    b = min(b, j)
                    blk = kept[:, t, off * D:(off + (KEEP[n][1] - a) * width) * D].rearrange(
                        "p (i w) -> p i w", w=width * D)
                    at = (j - 1 - a) * D
                    earlier = blk[:, 0:b - a, at:at + D]
                    last = nc.vector.tensor_tensor_reduce(
                        earlier,
                        stage[:, j % STAGE, t, a * D:b * D].rearrange("p (i d) -> p i d", d=D),
                        earlier, 1.0, 0.0, ALU.mult, ALU.add,
                        fm2_parts[:, t, m:m + 1])
                last.then_inc(s_fm2, 1)

            def lo(c):
                rows = chunk_rows(c)
                dve.wait_ge(s_hi, c + 1)
                nc.vector.tensor_tensor(dnn_lo[0:rows, c % HL_RING, :],
                                        turned[c % T_RING][0:rows, :],
                                        dnn_hi[0:rows, c % HL_RING, :].bitcast(F32),
                                        ALU.subtract).then_inc(s_lo, 1)

            dense_lo(0)
            dense_lo(1)
            for c in range(CHUNKS):
                if c >= 1:
                    lo(c - 1)
                for u in range(units_issued(c - 1), units_issued(c)):
                    j, t = divmod(u, BT)
                    if t == BT - 2 and DW_RING <= j + 1 < F:
                        dense_lo(j + 1)
                    make_dnn(u)
                    pairwise(u)
            lo(CHUNKS - 1)

            steps = [0]

            def step(instruction):
                steps[0] += 1
                instruction.then_inc(s_dstep, 1)
                dve.wait_ge(s_dstep, steps[0])

            dve.wait_ge(s_fm1, F)
            nc.vector.reduce_sum(fm1_sum[:], fm1_parts[:], AX_X).then_inc(s_dstep, 1)
            nc.vector.reduce_sum(fm2_sum[:], fm2_parts[:], AX_X).then_inc(s_dstep, 1)
            steps[0] = 2
            dve.wait_ge(s_dstep, 2)
            step(nc.vector.tensor_tensor(fm_sum[:], fm1_sum[:], fm2_sum[:], ALU.add))
            dve.wait_ge(s_first_ps, 1)
            step(nc.vector.tensor_tensor(fm_all[:], first_ps, fm_sum[:], ALU.add))
            dve.wait_ge(s_small_in, 16 * SMALL_LOADS)

            def statistics(n, src):
                step(nc.vector.bn_stats(stats[:, n, :], src))
                nc.vector.bn_aggr(mv[:, n, :], stats[:, n, :]).then_inc(s_var, 1)

            def batch_norm(a, b, params, which):
                cols = slice(a, b)
                r, v = rec[:, cols], ve[:, cols]
                dve.wait_ge(s_var, b)
                nc.vector.tensor_scalar(v, mv[:, cols, 1], EPS, None, ALU.add).then_inc(s_dstep, 1)
                steps[0] += 1
                dve.wait_ge(s_root, which)
                step(nc.vector.reciprocal(r, root[:, cols]))
                nc.vector.tensor_tensor(nwt[:, 0, cols], r, params[:, 0, :],
                                        ALU.mult).then_inc(s_dstep, 1)
                steps[0] += 1
                step(nc.vector.tensor_tensor(nwt[:, 1, cols], r, r, ALU.mult))
                step(nc.vector.scalar_tensor_tensor(out=nwt[:, 2, cols], in0=nwt[:, 1, cols],
                                                    scalar=-0.5, in1=v, op0=ALU.mult,
                                                    op1=ALU.mult))
                step(nc.vector.scalar_tensor_tensor(out=scale[:, cols], in0=nwt[:, 2, cols],
                                                    scalar=1.5, in1=nwt[:, 0, cols],
                                                    op0=ALU.add, op1=ALU.mult))
                for n in range(a, b):
                    nc.vector.scalar_tensor_tensor(
                        out=shift[:, n:n + 1], in0=scale[:, n:n + 1], scalar=mv[:, n, 0:1],
                        in1=params[:, 1, n - a:n - a + 1], op0=ALU.mult, op1=ALU.subtract,
                        reverse1=True).then_inc(s_affine, 1)

            for h in range(2):
                dve.wait_ge(s_acc, h + 1)
                statistics(h, acc[h][:])
            batch_norm(0, 2, bn1_sb, 2)
            dve.wait_ge(s_h2_ps, 1)
            statistics(2, h2_ps[:])
            batch_norm(2, 3, bn2_sb, 3)
            dve.wait_ge(s_z_ps, 1)
            nc.vector.tensor_tensor(z[:], z_ps, fm_all[:], ALU.add).then_inc(s_z, 1)

        @block.tensor
        def _(pe):
            def dense(u):
                j, t = divmod(u, BT)
                if t == 0:
                    pe.wait_ge(s_dw_lo, j + 1)
                if u >= R_RING:
                    pe.wait_ge(s_dnn, u - R_RING + 1)
                nc.tensor.matmul(dense_ps[u % R_RING][:, 0:FD], x_split[:, t * P:(t + 1) * P],
                                 dw[:, j % DW_RING, :], start=True, stop=True
                                 ).then_inc(s_dense, 1)

            def turn(c):
                rows = chunk_rows(c)
                at = c * P % (DNN_RING * FD)
                pe.wait_ge(s_dnn, units_for_chunk(c))
                if c >= T_RING:
                    pe.wait_ge(s_lo, c - T_RING + 1)
                for t in range(BT):
                    last = nc.tensor.transpose(turned[c % T_RING][0:rows, t * P:(t + 1) * P],
                                               dnn[:, t, at:at + rows], ident[:])
                last.then_inc(s_turned, 1)

            def multiply(c, ahead):
                rows = chunk_rows(c)
                slot, pair = c % HL_RING, (c // 2) % W_RING
                pe.wait_ge(s_lo, c + 1)
                pe.wait_ge(s_w_lo, c // 2 + 1)
                for h in range(2):
                    at = (c % 2) * H1 + h * P
                    for w, x in ((w_hi, dnn_hi), (w_lo, dnn_hi), (w_hi, dnn_lo)):
                        last = nc.tensor.matmul(acc[h][:], w[0:rows, pair, at:at + P],
                                                x[0:rows, slot, :], start=False,
                                                stop=(c == CHUNKS - 1 and x is dnn_lo))
                    for u in ahead[h::2]:
                        dense(u)
                    if c == CHUNKS - 1:
                        last.then_inc(s_acc, 1)
                if c < CHUNKS - 1:
                    last.then_inc(s_mult, 1)

            def start_accumulators():
                pe.wait_ge(s_b1_in, 16)
                pe.wait_ge(s_consts, 1)
                for h in range(2):
                    nc.tensor.matmul(acc[h][:], b1_row[:, h * P:(h + 1) * P], ones[:],
                                     start=True, stop=False)

            pe.wait_ge(s_x_lo, 2)
            def early_tail():
                pe.wait_ge(s_small_in, 16 * SMALL_LOADS)
                pe.wait_ge(s_lo, CHUNKS - T_RING + 1)
                nc.tensor.matmul(h2_ps[:], b2_row[:], ones[:], start=True, stop=False)
                for t in range(BT):
                    last = nc.tensor.matmul(first_ps[:, t:t + 1], x_rows[:, t * P:(t + 1) * P],
                                            fm_sb[:], start=True, stop=True)
                last.then_inc(s_first_ps, 1)

            for u in range(units_issued(0)):
                dense(u)
                if u == 1:
                    start_accumulators()
            pe.wait_ge(s_ident_in, 16)
            for c in range(CHUNKS + M_LAG):
                if c < CHUNKS:
                    turn(c)
                ahead = list(range(units_issued(c), units_issued(c + 1)))
                if c >= M_LAG:
                    multiply(c - M_LAG, ahead)
                else:
                    for u in ahead:
                        dense(u)
                if c == CHUNKS:
                    early_tail()

            for h in range(2):
                pe.wait_ge(s_h, h + 1)
                last = nc.tensor.matmul(h2_ps[:], w2_sb[:, h, :], h1[:, h, :], start=False,
                                        stop=(h == 1))
            last.then_inc(s_h2_ps, 1)
            pe.wait_ge(s_h, 3)
            for t in range(BT):
                last = nc.tensor.matmul(z_ps[:, t:t + 1], h2[:, 0, t * P:(t + 1) * P], wo_sb[:],
                                        start=True, stop=True)
            last.then_inc(s_z_ps, 1)


def kernel(r_X_dense, r_X_sparse, L0_rec_fm1_emb, L0_rec_bias, L0_rec_fm1_dense_W,
           L0_rec_fm1_dense_b, L0_rec_emb_tables, L0_rec_dense_W, L0_rec_dense_b, L0_rec_W1,
           L0_rec_b1, L0_rec_g1, L0_rec_beta1, L0_rec_W2, L0_rec_b2, L0_rec_g2, L0_rec_beta2,
           L0_rec_Wout, L0_rec_bout):
    import numpy as np
    import concourse.bacc as bacc
    from concourse.bass_utils import run_bass_kernel_spmd

    def a(x):
        return np.asarray(x)

    w1_k = a(L0_rec_W1).reshape(H1, F, F, D).transpose(2, 1, 3, 0).reshape(K, H1)
    dense_k = a(L0_rec_dense_W).reshape(F, F, D, ND).transpose(1, 0, 2, 3).reshape(K, ND)
    dense_b = a(L0_rec_dense_b).reshape(F, F, D).transpose(1, 0, 2).reshape(1, K)
    whole = K // P
    arrays = {
        "x_dense": np.concatenate([a(r_X_dense).T, np.ones((3, B), np.float32)]),
        "x_sparse": a(r_X_sparse).reshape(BT, P, F).transpose(1, 0, 2).reshape(P, BT * F),
        "table": np.concatenate([a(L0_rec_emb_tables).transpose(1, 0, 2).reshape(V, FD),
                                 a(L0_rec_fm1_emb)], axis=1),
        "dense_w": np.concatenate([dense_k.T, dense_b]),
        "w1": w1_k[:whole * P].reshape(whole, P, H1).transpose(1, 0, 2).reshape(P, whole * H1),
        "w1_last": w1_k[whole * P:],
        "w2": a(L0_rec_W2).T.reshape(2, P, H2).transpose(1, 0, 2),
        "b1": a(L0_rec_b1).reshape(1, H1),
        "b2": a(L0_rec_b2).reshape(1, H2),
        "bn1": np.stack([a(L0_rec_g1).reshape(2, P).T, a(L0_rec_beta1).reshape(2, P).T], axis=1),
        "bn2": np.stack([a(L0_rec_g2), a(L0_rec_beta2)], axis=1).reshape(P, 2, 1),
        "fm_col": np.concatenate([a(L0_rec_fm1_dense_W).reshape(ND), a(L0_rec_fm1_dense_b),
                                  a(L0_rec_bias), a(L0_rec_bout)]).reshape(NX, 1),
        "w_out": a(L0_rec_Wout).reshape(H2, 1),
        "ident_in": np.eye(P, dtype=np.float32),
    }
    arrays = {n: np.ascontiguousarray(x) for n, x in arrays.items()}
    nc = bacc.Bacc("TRN2", target_bir_lowering=False, num_devices=1)
    args = {n: nc.dram_tensor(f"in_{n}", x.shape, mybir.dt.from_np(x.dtype), kind="ExternalInput").ap()
            for n, x in arrays.items()}
    result = nc.dram_tensor("out_y", (P, BT), F32, kind="ExternalOutput").ap()
    build(nc, **args, out=result)
    r = run_bass_kernel_spmd(nc, [{f"in_{n}": x for n, x in arrays.items()}], core_ids=[0])
    return np.asarray(r.results[0]["out_y"]).T.reshape(B, 1)
```

```python
from contextlib import ExitStack

import concourse.bass as bass
from concourse import mybir

F32 = mybir.dt.float32
F32R = mybir.dt.float32r
I32 = mybir.dt.int32
ALU = mybir.AluOpType
ACT = mybir.ActivationFunctionType
AX_X = mybir.AxisListType.X

P = 128
F = 26
D = 16
V_FIELD = 1000
V = F * V_FIELD
FD = F * D
ROW = FD + 1
K = F * FD
H1, H2 = 256, 128
B = 512
BT = B // P
ND = 13
NA = ND + 1
NX = ND + 3
Q = 32
EPS = 1e-5

CHUNKS = -(-K // P)
PAIRS = -(-CHUNKS // 2)
UNITS = F * BT

STAGE = 5
DNN_RING = 4
T_RING = 4
R_RING = 2
HL_RING = 3
W_RING = 3
DW_RING = 2
DW_PARTS = 8
DVE_SPLITS = range(10)
LEAD = 8
M_LAG = 2
FILL = 5

KEEP, kept_vectors = [], 0
for a, b in ((0, 7), (7, 13), (13, 19), (19, 25)):
    KEEP.append((a, b, F - 1 - a, kept_vectors))
    kept_vectors += (b - a) * (F - 1 - a)
PIECES = [(j, n) for j in range(1, F) for n, blk in enumerate(KEEP) if blk[0] < j]
DW_FIRST = DW_RING * 2 * FD
HALVES = (slice(0, B // 2), slice(B // 2, B))
STACKED = (slice(0, P // 2), slice(P // 2, P))


def chunk_rows(c):
    return min(P, K - c * P)


def units_for_chunk(c):
    return BT * ((c * P + chunk_rows(c) - 1) // FD + 1)


def units_issued(c):
    return 0 if c < 0 else min(UNITS, c * UNITS * P // K + LEAD, BT + 2 * c)


def last_chunk_of_field(j):
    return (FD * (j + 1) - 1) // P


def tri_copies(j):
    return 2 * min(j + 1, F - 1)


def build(nc, x_dense, x_sparse, table, dense_first, dense_rest, dw_split, w1, w1_last, w2, b1, b2, bn1, bn2, fm_col, w_out,
          ident_in, out):
    ctx = ExitStack()
    with ctx:
        def sb(name, shape, dt=F32):
            return ctx.enter_context(nc.sbuf_tensor(name, shape, dt))

        def pb(name, shape):
            return ctx.enter_context(nc.psum_tensor(name, shape, F32))

        def sem(name):
            return ctx.enter_context(nc.semaphore(name))

        idx_in = sb("idx_in", [P, BT * F], I32)
        idx_off = sb("idx_off", [P, BT * F], I32)
        idx_sum = sb("idx_sum", [P, BT * F], I32)
        idx_wrap = sb("idx_wrap", [P, BT * F])
        idx_pos = sb("idx_pos", [P, BT * F])
        idx = sb("idx", [P, BT * F], I32)
        stage = sb("stage", [P, STAGE, BT, ROW])
        kept = sb("kept", [P, BT, kept_vectors * D])
        dnn = sb("dnn", [P, BT, DNN_RING * FD])
        fm2_parts = sb("fm2_parts", [P, BT, len(PIECES)])
        fm1_parts = sb("fm1_parts", [P, BT, F])
        dnn_hi = sb("dnn_hi", [P, HL_RING, B], F32R)
        dnn_lo = sb("dnn_lo", [P, HL_RING, B], F32R)
        w_raw = sb("w_raw", [P, W_RING, 2 * H1])
        w_hi = sb("w_hi", [P, W_RING, 2 * H1], F32R)
        w_lo = sb("w_lo", [P, W_RING, 2 * H1], F32R)
        dw = sb("dw", [P, DW_RING, 2 * FD], F32R)
        dw_flat = dw[:].rearrange("p m k -> p (m k)")
        dw_raw = stage[:, STAGE - 1].rearrange("p t k -> p (t k)")
        at = KEEP[2][3] * D
        rest_raw, rest_hi, rest_lo = (kept[0:NA * DW_PARTS, t, at:at + (K - DW_FIRST) // DW_PARTS]
                                   for t in range(3))
        x_raw = dnn[:, BT - 1, DNN_RING * FD - B:]
        x_split = sb("x_split", [P, B], F32R)
        x_rows = sb("x_rows", [NX, B])
        ident = sb("ident", [P, P])
        b1_row = sb("b1_row", [1, H1])
        b1_hi = sb("b1_hi", [1, H1], F32R)
        b1_lo = sb("b1_lo", [1, H1], F32R)
        b2_row = sb("b2_row", [1, H2])
        bn1_sb = sb("bn1_sb", [P, 2, 2])
        bn2_sb = sb("bn2_sb", [P, 2, 1])
        fm_sb = sb("fm_sb", [NX, 1])
        w2_sb = sb("w2_sb", [P, 2, H2])
        wo_sb = sb("wo_sb", [P, 1])
        h1 = dnn[:, 0:2, 0:B]
        h2 = dnn[:, 2:3, 0:B]
        stats1 = sb("stats1", [P, 2, 6])
        stats2 = sb("stats2", [P, 2, 6])
        mv = sb("mv", [P, 3, 2])
        ve = sb("ve", [P, 3])
        rec = sb("rec", [P, 3])
        root = sb("root", [P, 3])
        nwt = sb("nwt", [P, 3, 3])
        scale = sb("scale", [P, 3])
        shift = sb("shift", [P, 3])
        fm1_sum = sb("fm1_sum", [P, BT])
        fm2_sum = sb("fm2_sum", [P, BT])
        fm_sum = sb("fm_sum", [P, BT])
        fm_all = sb("fm_all", [P, BT])
        eps = sb("eps", [P, 1])
        z = sb("z", [P, BT])
        warm = sb("warm", [P, 2])
        y = sb("y", [P, BT])

        acc = [pb(f"acc{h}", [P, B]) for h in range(2)]
        turned = [pb(f"turned{n}", [P, B]) for n in range(T_RING)]
        dense_ps = [pb(f"dense_ps{n}", [P, B]) for n in range(R_RING)]
        h2_ps = [turned[(CHUNKS + n) % T_RING][:, 0:B // 2] for n in range(2)]
        z_ps = dense_ps[0][:, 0:BT]
        first_ps = dense_ps[1][:, 0:BT]

        s_idx_in = sem("s_idx_in")
        s_x_in = sem("s_x_in")
        s_b1_in = sem("s_b1_in")
        s_ident_in = sem("s_ident_in")
        s_small_in = sem("s_small_in")
        s_zeroed = sem("s_zeroed")
        s_consts = sem("s_consts")
        s_off = sem("s_off")
        s_idx_sum = sem("s_idx_sum")
        s_idx_step = sem("s_idx_step")
        s_idx = sem("s_idx")
        s_b1_hi = sem("s_b1_hi")
        s_b1_lo = sem("s_b1_lo")
        s_x_hi = sem("s_x_hi")
        s_x_lo = sem("s_x_lo")
        s_gathered = [[sem(f"s_gathered{n}_{t}") for t in range(BT)] for n in range(STAGE)]
        s_w_raw = [sem(f"s_w_raw{n}") for n in range(W_RING)]
        s_dw_raw = [sem(f"s_dw_raw{n}") for n in range(DW_RING)]
        s_dw = [sem(f"s_dw{n}") for n in range(DW_RING)]
        s_rest_raw = sem("s_rest_raw")
        s_rest_hi = sem("s_rest_hi")
        s_rest_lo = sem("s_rest_lo")
        s_rest_out = sem("s_rest_out")
        s_w_hi = sem("s_w_hi")
        s_w_lo_pool = sem("s_w_lo_pool")
        s_w_lo_dve = sem("s_w_lo_dve")
        s_dw_hi = sem("s_dw_hi")
        s_dw_lo = sem("s_dw_lo")
        s_dense = sem("s_dense")
        s_dnn = sem("s_dnn")
        s_fm2 = sem("s_fm2")
        s_tri = sem("s_tri")
        s_fm1 = sem("s_fm1")
        s_turned = sem("s_turned")
        s_hi = sem("s_hi")
        s_lo = sem("s_lo")
        s_mult = sem("s_mult")
        s_warm = sem("s_warm")
        s_acc = sem("s_acc")
        s_first_ps = sem("s_first_ps")
        s_var = sem("s_var")
        s_root = sem("s_root")
        s_affine = sem("s_affine")
        s_h = sem("s_h")
        s_h2_ps = sem("s_h2_ps")
        s_z_ps = sem("s_z_ps")
        s_z = sem("s_z")
        s_y = sem("s_y")
        s_out = sem("s_out")
        s_dstep = sem("s_dstep")

        SMALL_LOADS = 7
        W_LAST = (CHUNKS - 1) // 2

        def wait_w_lo(engine, p):
            on_dve = sum(n <= p for n in DVE_SPLITS)
            if p in DVE_SPLITS:
                engine.wait_ge(s_w_lo_dve, on_dve)
            else:
                engine.wait_ge(s_w_lo_pool, p + 1 - on_dve)

        block = ctx.enter_context(nc.Block())

        @block.sync
        def _(sp):
            sp.dma_start(idx_in[:], x_sparse).then_inc(s_idx_in, 16)
            sp.dma_start(rest_raw, dense_rest).then_inc(s_rest_raw, 16)

            def load_first_dense_w(m):
                cols = slice(2 * m * FD, 2 * (m + 1) * FD)
                for q in range(4):
                    sp.dma_start(dw_raw[Q * q:Q * q + NA, cols], dense_first[:, cols]
                                 ).then_inc(s_dw_raw[m], 16)

            def load_dense_w(m):
                slot = m % DW_RING
                sp.wait_ge(s_dense, 2 * BT * (m - DW_RING + 1))
                for q in range(4):
                    sp.dma_start(dw[Q * q:Q * q + NA, slot, :].bitcast(F32),
                                 dw_split[q // 2, :, 2 * m * FD - DW_FIRST:
                                          2 * (m + 1) * FD - DW_FIRST]
                                 ).then_inc(s_dw[slot], 16)

            def load_w1(p):
                slot = p % W_RING
                if p >= W_RING:
                    wait_w_lo(sp, p - W_RING)
                if p == W_LAST:
                    for rows in STACKED:
                        sp.dma_start(w_raw[rows, slot, 0:H1], w1_last).then_inc(s_w_raw[slot], 16)
                else:
                    sp.dma_start(w_raw[:, slot, :], w1[:, 2 * p * H1:(2 * p + 2) * H1]
                                 ).then_inc(s_w_raw[slot], 16)

            sp.wait_ge(s_zeroed, 1)
            for q in range(4):
                sp.dma_start(x_raw[Q * q:Q * q + NA, :], x_dense[NX - NA:NX, :]).then_inc(s_x_in, 16)
            sp.wait_ge(s_zeroed, 2)
            load_first_dense_w(0)
            sp.dma_start(b1_row[:], b1).then_inc(s_b1_in, 16)
            sp.dma_start(ident[:], ident_in).then_inc(s_ident_in, 16)
            sp.wait_ge(s_zeroed, 3)
            load_first_dense_w(1)
            load_w1(0)
            sp.wait_ge(s_gathered[1][0], 16)
            load_w1(1)
            load_w1(2)
            sp.wait_ge(s_gathered[2][1], 16)
            sp.wait_ge(s_rest_hi, 1)
            sp.dma_start(dw_split[0].rearrange("r (s k) -> (r s) k", s=DW_PARTS), rest_hi
                         ).then_inc(s_rest_out, 16)
            sp.wait_ge(s_rest_lo, 1)
            sp.dma_start(dw_split[1].rearrange("r (s k) -> (r s) k", s=DW_PARTS), rest_lo
                         ).then_inc(s_rest_out, 16)
            sp.wait_ge(s_rest_out, 32)
            m = DW_RING
            for p in range(W_RING, PAIRS):
                if m < F // 2 and 2 * m * FD < (2 * p + 5) * P:
                    load_dense_w(m)
                    m += 1
                load_w1(p)
                if p == PAIRS // 2:
                    for t, src in ((x_rows, x_dense), (b2_row, b2), (bn1_sb, bn1), (bn2_sb, bn2),
                                   (fm_sb, fm_col), (w2_sb, w2), (wo_sb, w_out)):
                        sp.dma_start(t[:], src).then_inc(s_small_in, 16)
            sp.wait_ge(s_y, 1)
            sp.dma_start(out, y[:]).then_inc(s_out, 16)
            sp.wait_ge(s_out, 16)

        @block.gpsimd
        def _(pool):
            nc.gpsimd.iota(idx_off[:].rearrange("p (t f) -> p t f", f=F), pattern=[[0, BT], [V_FIELD, F]], base=0,
                           channel_multiplier=0).then_inc(s_off, 1)
            pool.wait_ge(s_off, 1)
            pool.wait_ge(s_idx_in, 16)
            nc.gpsimd.tensor_tensor(idx_sum[:], idx_in[:], idx_off[:], ALU.add).then_inc(s_idx_sum, 1)
            pool.wait_ge(s_idx, 1)

            def gather(j):
                slot = j % STAGE
                if j >= STAGE:
                    done = j - STAGE + 1
                    pool.wait_ge(s_dnn, BT * done)
                    if done > 1:
                        pool.wait_ge(s_fm2, BT * (done - 1))
                    pool.wait_ge(s_tri, tri_copies(done - 1))
                    pool.wait_ge(s_fm1, done)
                if j == STAGE - 1:
                    pool.wait_ge(s_dw_hi, 2 * DW_RING)
                    pool.wait_ge(s_dw_lo, 2 * DW_RING)
                for t in range(BT):
                    col = t * F + j
                    nc.gpsimd.indirect_dma_start(
                        out=stage[:, slot, t, :], out_offset=None, in_=table,
                        in_offset=bass.IndirectOffsetOnAxis(ap=idx[:, col:col + 1], axis=0),
                    ).then_inc(s_gathered[slot][t], 16)

            def split_w1(p):
                if p in DVE_SPLITS:
                    return
                slot = p % W_RING
                cols = H1 if p == W_LAST else 2 * H1
                pool.wait_ge(s_w_hi, p + 1)
                nc.gpsimd.tensor_tensor(w_lo[:, slot, 0:cols], w_raw[:, slot, 0:cols],
                                        w_hi[:, slot, 0:cols].bitcast(F32), ALU.subtract
                                        ).then_inc(s_w_lo_pool, 1)

            p = 0
            for j in range(F):
                gather(j)
                while p < PAIRS and (p < min(W_RING, j)
                                     or 2 * p * P < (j - STAGE + 1) * FD + 3 * P):
                    split_w1(p)
                    p += 1
            while p < PAIRS:
                split_w1(p)
                p += 1

        @block.scalar
        def _(act):
            act.wait_ge(s_x_in, 64)
            nc.scalar.copy(x_split[:], x_raw).then_inc(s_x_hi, 1)

            def dense_hi(j):
                act.wait_ge(s_dw_raw[j // 2], 64)
                nc.scalar.copy(dw_flat[:, j * FD:(j + 1) * FD], dw_raw[:, j * FD:(j + 1) * FD]
                               ).then_inc(s_dw_hi, 1)

            def w1_hi(p):
                slot = p % W_RING
                cols, loads = (H1, 2) if p == W_LAST else (2 * H1, 1)
                act.wait_ge(s_w_raw[slot], 16 * (p // W_RING + loads))
                if p >= W_RING:
                    act.wait_ge(s_mult, 2 * (p - W_RING + 1))
                nc.scalar.copy(w_hi[:, slot, 0:cols], w_raw[:, slot, 0:cols]
                               ).then_inc(s_w_hi, 1)

            def keep(j):
                slot = j % STAGE
                for t in range(BT):
                    act.wait_ge(s_gathered[slot][t], 16 * (j // STAGE + 1))
                nc.scalar.copy(fm1_parts[:, :, j], stage[:, slot, :, FD]).then_inc(s_fm1, 1)
                if j == F - 1:
                    return
                a, _, width, off = next(blk for blk in KEEP if blk[0] <= j < blk[1])
                at = (off + (j - a) * width + (j - a)) * D
                if j == KEEP[2][0]:
                    act.wait_ge(s_rest_out, 32)
                n = (F - 1 - j) * D
                for t in (0, 2):
                    nc.scalar.copy(kept[:, t:t + 2, at:at + n],
                                   stage[:, slot, t:t + 2, (j + 1) * D:FD]).then_inc(s_tri, 1)

            def hi(c):
                rows = chunk_rows(c)
                act.wait_ge(s_turned, c + 1)
                if c >= HL_RING:
                    act.wait_ge(s_mult, c - HL_RING + 1)
                nc.scalar.copy(dnn_hi[0:rows, c % HL_RING, :], turned[c % T_RING][0:rows, :]
                               ).then_inc(s_hi, 1)

            dense_hi(0)
            dense_hi(1)
            act.wait_ge(s_b1_in, 16)
            nc.scalar.copy(b1_hi[:], b1_row[:]).then_inc(s_b1_hi, 1)
            act.wait_ge(s_rest_raw, 16)
            nc.scalar.copy(rest_hi.bitcast(F32R), rest_raw).then_inc(s_rest_hi, 1)
            keep(0)
            w1_hi(0)
            p, f = 1, 1
            for c in range(CHUNKS):
                hi(c)
                if c < 2:
                    dense_hi(c + 2)
                while f < F and BT * (f + 1) <= units_issued(c):
                    keep(f)
                    f += 1
                if p < PAIRS and 2 * p <= c + 2:
                    w1_hi(p)
                    p += 1

            def normalise(n, src, dst):
                nc.scalar.activation(dst, src, ACT.Relu, bias=shift[:, n:n + 1],
                                     scale=scale[:, n:n + 1]).then_inc(s_h, 1)

            act.wait_ge(s_consts, 1)
            nc.scalar.activation(warm[:, 0:1], eps[:], ACT.Sqrt).then_inc(s_warm, 1)

            def deviation(n):
                act.wait_ge(s_var, n + 1)
                nc.scalar.activation(root[:, n:n + 1], mv[:, n, 1:2], ACT.Sqrt, bias=eps[:]
                                     ).then_inc(s_root, 1)

            deviation(0)
            deviation(1)
            for h in range(2):
                act.wait_ge(s_affine, h + 1)
                for cols in HALVES:
                    normalise(h, acc[h][:, cols], h1[:, h, cols])
            deviation(2)
            nc.scalar.activation(warm[:, 1:2], eps[:], ACT.Sigmoid).then_inc(s_warm, 1)
            act.wait_ge(s_affine, 3)
            for t in range(BT):
                half, at = divmod(t * P, B // 2)
                normalise(2, h2_ps[half][:, at:at + P], h2[:, 0, t * P:(t + 1) * P])
            act.wait_ge(s_z, 1)
            nc.scalar.activation(y[:], z[:], ACT.Sigmoid).then_inc(s_y, 1)

        @block.vector
        def _(dve):
            nc.vector.memset(x_raw, 0.0).then_inc(s_zeroed, 1)
            for m in range(DW_RING):
                nc.vector.memset(dw_raw[:, 2 * m * FD:2 * (m + 1) * FD], 0.0
                                 ).then_inc(s_zeroed, 1)
            dve.wait_ge(s_idx_sum, 1)
            nc.vector.tensor_scalar(idx_wrap[:], idx_sum[:], 0.0, float(V), ALU.is_lt, ALU.mult
                                    ).then_inc(s_idx_step, 1)
            dve.wait_ge(s_idx_step, 1)
            nc.vector.tensor_tensor(idx_pos[:], idx_sum[:], idx_wrap[:], ALU.add
                                    ).then_inc(s_idx_step, 1)
            dve.wait_ge(s_idx_step, 2)
            nc.vector.tensor_scalar(idx[:], idx_pos[:], 0.0, float(V - 1), ALU.max, ALU.min
                                    ).then_inc(s_idx, 1)
            nc.vector.memset(eps[:], EPS).then_inc(s_consts, 1)
            dve.wait_ge(s_x_hi, 1)
            for q in (1, 3):
                rows = slice(Q * q, Q * (q + 1))
                nc.vector.tensor_tensor(x_split[rows, :], x_raw[rows, :],
                                        x_split[rows, :].bitcast(F32), ALU.subtract
                                        ).then_inc(s_x_lo, 1)

            def dense_lo(j):
                rows, cols = slice(2 * Q, 4 * Q), slice(j * FD, (j + 1) * FD)
                dve.wait_ge(s_dw_hi, j + 1)
                nc.vector.tensor_tensor(dw_flat[rows, cols], dw_raw[rows, cols],
                                        dw_flat[rows, cols].bitcast(F32), ALU.subtract
                                        ).then_inc(s_dw_lo, 1)

            def split_w1(p):
                slot = p % W_RING
                dve.wait_ge(s_w_hi, p + 1)
                nc.vector.tensor_tensor(w_lo[:, slot, :], w_raw[:, slot, :],
                                        w_hi[:, slot, :].bitcast(F32), ALU.subtract
                                        ).then_inc(s_w_lo_dve, 1)

            def make_dnn(u):
                j, t = divmod(u, BT)
                slot = j % STAGE
                dve.wait_ge(s_dense, u + 1)
                dve.wait_ge(s_gathered[slot][t], 16 * (j // STAGE + 1))
                if t == 0 and j >= DNN_RING:
                    dve.wait_ge(s_turned, last_chunk_of_field(j - DNN_RING) + 1)
                at = (j % DNN_RING) * FD
                nc.vector.scalar_tensor_tensor(
                    out=dnn[:, t, at:at + FD], in0=dense_ps[u % R_RING][:, 0:FD], scalar=0.0,
                    in1=stage[:, slot, t, 0:FD], op0=ALU.max, op1=ALU.add).then_inc(s_dnn, 1)

            def pairwise(u):
                j, t = divmod(u, BT)
                if j == 0:
                    return
                if t == 0:
                    dve.wait_ge(s_tri, tri_copies(j - 1))
                for m, (jj, n) in enumerate(PIECES):
                    if jj != j:
                        continue
                    a, b, width, off = KEEP[n]
                    b = min(b, j)
                    blk = kept[:, t, off * D:(off + (KEEP[n][1] - a) * width) * D].rearrange(
                        "p (i w) -> p i w", w=width * D)
                    at = (j - 1 - a) * D
                    earlier = blk[:, 0:b - a, at:at + D]
                    last = nc.vector.tensor_tensor_reduce(
                        earlier,
                        stage[:, j % STAGE, t, a * D:b * D].rearrange("p (i d) -> p i d", d=D),
                        earlier, 1.0, 0.0, ALU.mult, ALU.add,
                        fm2_parts[:, t, m:m + 1])
                last.then_inc(s_fm2, 1)

            def lo(c):
                rows = chunk_rows(c)
                dve.wait_ge(s_hi, c + 1)
                to = (dnn_hi[STACKED[1], c % HL_RING, :] if c == CHUNKS - 1
                      else dnn_lo[:, c % HL_RING, :])
                nc.vector.tensor_tensor(to,
                                        turned[c % T_RING][0:rows, :],
                                        dnn_hi[0:rows, c % HL_RING, :].bitcast(F32),
                                        ALU.subtract).then_inc(s_lo, 1)

            dense_lo(0)
            dve.wait_ge(s_b1_hi, 1)
            nc.vector.tensor_tensor(b1_lo[:], b1_row[:], b1_hi[:].bitcast(F32), ALU.subtract
                                    ).then_inc(s_b1_lo, 1)
            for c in range(CHUNKS):
                if c > FILL:
                    lo(c - 1)
                for u in range(units_issued(c - 1), units_issued(c)):
                    j, t = divmod(u, BT)
                    if t == 2 and j + 1 < 2 * DW_RING:
                        dense_lo(j + 1)
                    if u == BT:
                        dve.wait_ge(s_rest_hi, 1)
                        nc.vector.tensor_tensor(rest_lo.bitcast(F32R), rest_raw, rest_hi,
                                                ALU.subtract).then_inc(s_rest_lo, 1)
                    make_dnn(u)
                    pairwise(u)
                if 1 <= c <= FILL:
                    lo(c - 1)
                if c % 2 == 0 and c // 2 in DVE_SPLITS:
                    split_w1(c // 2)
            lo(CHUNKS - 1)

            steps = [0]

            def step(instruction):
                steps[0] += 1
                instruction.then_inc(s_dstep, 1)
                dve.wait_ge(s_dstep, steps[0])

            dve.wait_ge(s_fm1, F)
            nc.vector.reduce_sum(fm1_sum[:], fm1_parts[:], AX_X).then_inc(s_dstep, 1)
            nc.vector.reduce_sum(fm2_sum[:], fm2_parts[:], AX_X).then_inc(s_dstep, 1)
            steps[0] = 2
            dve.wait_ge(s_dstep, 2)
            step(nc.vector.tensor_tensor(fm_sum[:], fm1_sum[:], fm2_sum[:], ALU.add))
            dve.wait_ge(s_small_in, 16 * SMALL_LOADS)

            def batch_norm(a, b, params):
                cols = slice(a, b)
                r, v = rec[:, cols], ve[:, cols]
                dve.wait_ge(s_var, b)
                nc.vector.tensor_scalar(v, mv[:, cols, 1], EPS, None, ALU.add).then_inc(s_dstep, 1)
                steps[0] += 1
                dve.wait_ge(s_root, b)
                step(nc.vector.reciprocal(r, root[:, cols]))
                nc.vector.tensor_tensor(nwt[:, 0, cols], r, params[:, 0, :],
                                        ALU.mult).then_inc(s_dstep, 1)
                steps[0] += 1
                step(nc.vector.tensor_tensor(nwt[:, 1, cols], r, r, ALU.mult))
                step(nc.vector.scalar_tensor_tensor(out=nwt[:, 2, cols], in0=nwt[:, 1, cols],
                                                    scalar=-0.5, in1=v, op0=ALU.mult,
                                                    op1=ALU.mult))
                step(nc.vector.scalar_tensor_tensor(out=scale[:, cols], in0=nwt[:, 2, cols],
                                                    scalar=1.5, in1=nwt[:, 0, cols],
                                                    op0=ALU.add, op1=ALU.mult))
                for n in range(a, b):
                    nc.vector.scalar_tensor_tensor(
                        out=shift[:, n:n + 1], in0=scale[:, n:n + 1], scalar=mv[:, n, 0:1],
                        in1=params[:, 1, n - a:n - a + 1], op0=ALU.mult, op1=ALU.subtract,
                        reverse1=True).then_inc(s_affine, 1)

            for h in range(2):
                dve.wait_ge(s_acc, h + 1)
                step(nc.vector.bn_stats(stats1[:, h, :], acc[h][:]))
                nc.vector.bn_aggr(mv[:, h, :], stats1[:, h, :]).then_inc(s_var, 1)
            batch_norm(0, 2, bn1_sb)
            dve.wait_ge(s_first_ps, 1)
            nc.vector.tensor_tensor(fm_all[:], first_ps, fm_sum[:], ALU.add).then_inc(s_dstep, 1)
            steps[0] += 1
            for n in range(2):
                dve.wait_ge(s_h2_ps, n + 1)
                nc.vector.bn_stats(stats2[:, n, :], h2_ps[n]).then_inc(s_dstep, 1)
            steps[0] += 2
            dve.wait_ge(s_dstep, steps[0])
            nc.vector.bn_aggr(mv[:, 2, :], stats2[:]).then_inc(s_var, 1)
            batch_norm(2, 3, bn2_sb)
            dve.wait_ge(s_z_ps, 1)
            nc.vector.tensor_tensor(z[:], z_ps, fm_all[:], ALU.add).then_inc(s_z, 1)

        @block.tensor
        def _(pe):
            def dense(u):
                j, t = divmod(u, BT)
                m = j // 2
                if t == 0 and m < DW_RING:
                    pe.wait_ge(s_dw_lo, j + 1)
                elif t == 0 and j % 2 == 0:
                    pe.wait_ge(s_dw[m % DW_RING], 64 * (m // DW_RING))
                if u >= R_RING:
                    pe.wait_ge(s_dnn, u - R_RING + 1)
                nc.tensor.matmul(dense_ps[u % R_RING][:, 0:FD], x_split[:, t * P:(t + 1) * P],
                                 dw[:, m % DW_RING, j % 2 * FD:(j % 2 + 1) * FD],
                                 start=True, stop=True
                                 ).then_inc(s_dense, 1)

            def turn(c):
                rows = chunk_rows(c)
                at = c * P % (DNN_RING * FD)
                pe.wait_ge(s_dnn, units_for_chunk(c))
                if c >= T_RING:
                    pe.wait_ge(s_lo, c - T_RING + 1)
                for t in range(BT):
                    last = nc.tensor.transpose(turned[c % T_RING][0:rows, t * P:(t + 1) * P],
                                               dnn[:, t, at:at + rows], ident[:])
                last.then_inc(s_turned, 1)

            def multiply(c, halves, ahead=()):
                rows = chunk_rows(c)
                slot, pair = c % HL_RING, (c // 2) % W_RING
                pe.wait_ge(s_lo, c + 1)
                wait_w_lo(pe, c // 2)
                for h in halves:
                    at = (c % 2) * H1 + h * P
                    if c == CHUNKS - 1:
                        nc.tensor.matmul(acc[h][:], w_hi[:, pair, at:at + P], dnn_hi[:, slot, :],
                                         start=False, stop=False)
                        last = nc.tensor.matmul(acc[h][:], w_lo[0:rows, pair, at:at + P],
                                                dnn_hi[0:rows, slot, :], start=False, stop=True)
                        continue
                    for w, x in ((w_hi, dnn_hi), (w_lo, dnn_hi), (w_hi, dnn_lo)):
                        last = nc.tensor.matmul(acc[h][:], w[:, pair, at:at + P], x[:, slot, :],
                                                start=False, stop=False)
                    for u in ahead[h::2]:
                        dense(u)
                return last

            def start_accumulator(h):
                pe.wait_ge(s_b1_lo, 1)
                for row in (b1_hi, b1_lo):
                    nc.tensor.matmul(acc[h][:], row[:, h * P:(h + 1) * P], x_split[0:1, :],
                                     start=row is b1_hi, stop=False)

            def start_outputs():
                pe.wait_ge(s_small_in, 16 * SMALL_LOADS)
                for n, cols in enumerate(HALVES):
                    nc.tensor.matmul(h2_ps[n], b2_row[:], x_rows[0:1, cols], start=True,
                                     stop=False)
                for t in range(BT):
                    last = nc.tensor.matmul(first_ps[:, t:t + 1], x_rows[:, t * P:(t + 1) * P],
                                            fm_sb[:], start=True, stop=True)
                last.then_inc(s_first_ps, 1)

            pe.wait_ge(s_x_lo, 2)
            for u in range(units_issued(0)):
                dense(u)
                if u % R_RING == R_RING - 1 and u // R_RING < 2:
                    start_accumulator(u // R_RING)
            pe.wait_ge(s_ident_in, 16)
            for c in range(CHUNKS):
                turn(c)
                ahead = list(range(units_issued(c), units_issued(c + 1)))
                if c >= M_LAG:
                    multiply(c - M_LAG, (0, 1), ahead).then_inc(s_mult, 1)
                else:
                    for u in ahead:
                        dense(u)
            for h in range(2):
                for c in range(CHUNKS - M_LAG, CHUNKS):
                    last = multiply(c, (h,))
                last.then_inc(s_acc, 1)
            start_outputs()

            for h in range(2):
                for n, cols in enumerate(HALVES):
                    pe.wait_ge(s_h, 2 * h + n + 1)
                    last = nc.tensor.matmul(h2_ps[n], w2_sb[:, h, :], h1[:, h, cols],
                                            start=False, stop=(h == 1))
                    if h == 1:
                        last.then_inc(s_h2_ps, 1)
            for t in range(BT):
                pe.wait_ge(s_h, 4 + t + 1)
                last = nc.tensor.matmul(z_ps[:, t:t + 1], h2[:, 0, t * P:(t + 1) * P], wo_sb[:],
                                        start=True, stop=True)
            last.then_inc(s_z_ps, 1)


def kernel(r_X_dense, r_X_sparse, L0_rec_fm1_emb, L0_rec_bias, L0_rec_fm1_dense_W,
           L0_rec_fm1_dense_b, L0_rec_emb_tables, L0_rec_dense_W, L0_rec_dense_b, L0_rec_W1,
           L0_rec_b1, L0_rec_g1, L0_rec_beta1, L0_rec_W2, L0_rec_b2, L0_rec_g2, L0_rec_beta2,
           L0_rec_Wout, L0_rec_bout):
    import numpy as np
    import concourse.bacc as bacc
    from concourse.bass_utils import run_bass_kernel_spmd

    def a(x):
        return np.asarray(x)

    w1_k = a(L0_rec_W1).reshape(H1, F, F, D).transpose(2, 1, 3, 0).reshape(K, H1)
    dense_k = a(L0_rec_dense_W).reshape(F, F, D, ND).transpose(1, 0, 2, 3).reshape(K, ND)
    dense_b = a(L0_rec_dense_b).reshape(F, F, D).transpose(1, 0, 2).reshape(1, K)
    dense_w = np.concatenate([dense_b, dense_k.T])
    whole = K // P
    arrays = {
        "x_dense": np.concatenate([np.ones((3, B), np.float32), a(r_X_dense).T]),
        "x_sparse": a(r_X_sparse).reshape(BT, P, F).transpose(1, 0, 2).reshape(P, BT * F),
        "table": np.concatenate([a(L0_rec_emb_tables).transpose(1, 0, 2).reshape(V, FD),
                                 a(L0_rec_fm1_emb)], axis=1),
        "dense_first": dense_w[:, :DW_FIRST],
        "dense_rest": dense_w[:, DW_FIRST:].reshape(NA * DW_PARTS, -1),
        "w1": w1_k[:whole * P].reshape(whole, P, H1).transpose(1, 0, 2).reshape(P, whole * H1),
        "w1_last": w1_k[whole * P:],
        "w2": a(L0_rec_W2).T.reshape(2, P, H2).transpose(1, 0, 2),
        "b1": a(L0_rec_b1).reshape(1, H1),
        "b2": a(L0_rec_b2).reshape(1, H2),
        "bn1": np.stack([a(L0_rec_g1).reshape(2, P).T, a(L0_rec_beta1).reshape(2, P).T], axis=1),
        "bn2": np.stack([a(L0_rec_g2), a(L0_rec_beta2)], axis=1).reshape(P, 2, 1),
        "fm_col": np.concatenate([a(L0_rec_fm1_dense_b), a(L0_rec_bias), a(L0_rec_bout),
                                  a(L0_rec_fm1_dense_W).reshape(ND)]).reshape(NX, 1),
        "w_out": a(L0_rec_Wout).reshape(H2, 1),
        "ident_in": np.eye(P, dtype=np.float32),
    }
    arrays = {n: np.ascontiguousarray(x) for n, x in arrays.items()}
    nc = bacc.Bacc("TRN2", target_bir_lowering=False, num_devices=1)
    args = {n: nc.dram_tensor(f"in_{n}", x.shape, mybir.dt.from_np(x.dtype), kind="ExternalInput").ap()
            for n, x in arrays.items()}
    args["dw_split"] = nc.dram_tensor("dw_split", (2, NA, K - DW_FIRST), F32, kind="Internal").ap()
    result = nc.dram_tensor("out_y", (P, BT), F32, kind="ExternalOutput").ap()
    build(nc, **args, out=result)
    r = run_bass_kernel_spmd(nc, [{f"in_{n}": x for n, x in arrays.items()}], core_ids=[0])
    return np.asarray(r.results[0]["out_y"]).T.reshape(B, 1)
```
